# Optimizing a Trainium2 kernel written in Bass

```python
import numpy as np
import jax
import jax.numpy as jnp

def _softmax(x, axis=-1):
    return jax.nn.softmax(x, axis=axis)

def _gelu(x):
    return jax.nn.gelu(x, approximate=True)

def _silu(x):
    return jax.nn.silu(x)

def _sigmoid(x):
    return jax.nn.sigmoid(x)

def _layernorm(x, axis=-1, eps=1e-05):
    m = jnp.mean(x, axis=axis, keepdims=True)
    v = jnp.var(x, axis=axis, keepdims=True)
    return (x - m) / jnp.sqrt(v + eps)

def _scatter_add(tgt, idx, src, axis=0):
    return tgt.at[idx].add(src)

def _segment_sum(src, seg, n):
    return jax.ops.segment_sum(src, seg, n)
kernel_name = 'mk_seq_postln_d1_jaxref_r8_8ce2a7'

def setup_inputs(seed: int=0):
    np.random.seed(seed)
    _w = jnp.asarray

    def _L0_attn_setup():
        import jax, jax.numpy as jnp
        import numpy as np
        H = 16

        def _split_heads(x, h):
            B, T, D = x.shape
            return x.reshape(B, T, h, D // h).transpose(0, 2, 1, 3)
        key = jax.random.key(seed)
        ks = jax.random.split(key, 7)
        B, T, D = (2, 256, 256)
        s = 0.02
        return {'x': jax.random.normal(ks[0], (B, T, D), dtype=jnp.float32), 'Wq1': jax.random.normal(ks[1], (D, D), dtype=jnp.float32) * s, 'Wq2': jax.random.normal(ks[2], (D, D), dtype=jnp.float32) * s, 'Wk': jax.random.normal(ks[3], (D, D), dtype=jnp.float32) * s, 'Wv': jax.random.normal(ks[4], (D, D), dtype=jnp.float32) * s, 'Wlam': jax.random.normal(ks[5], (D, H), dtype=jnp.float32) * s, 'Wo': jax.random.normal(ks[6], (D, D), dtype=jnp.float32) * s}
    _L0_attn_in = _L0_attn_setup()

    def _L0_ffn_setup():
        import jax, jax.numpy as jnp
        import numpy as np
        HIDDEN = 256
        INTER = 1024
        MOE_INTER = 128
        N_ROUTED = 8
        NUM_LOCAL = 8
        TOP_K = 2
        B, S = (4, 256)

        def _mlp(x, gw, uw, dw):
            g = x @ gw.T
            u = x @ uw.T
            return g * jax.nn.sigmoid(g) * u @ dw.T
        key = jax.random.key(seed)
        ks = jax.random.split(key, 8)
        std = 0.02
        return {'hidden_states': jax.random.normal(ks[0], (B, S, HIDDEN), jnp.float32), 'router_weight': jax.random.normal(ks[1], (N_ROUTED, HIDDEN), jnp.float32) * std, 'sh_gate': jax.random.normal(ks[2], (INTER, HIDDEN), jnp.float32) * std, 'sh_up': jax.random.normal(ks[3], (INTER, HIDDEN), jnp.float32) * std, 'sh_down': jax.random.normal(ks[4], (HIDDEN, INTER), jnp.float32) * std, 'r_gate': jax.random.normal(ks[5], (MOE_INTER, HIDDEN), jnp.float32) * std, 'r_up': jax.random.normal(ks[6], (MOE_INTER, HIDDEN), jnp.float32) * std, 'r_down': jax.random.normal(ks[7], (HIDDEN, MOE_INTER), jnp.float32) * std}
    _L0_ffn_in = _L0_ffn_setup()
    _d = {'L0_attn_x': _L0_attn_in['x'], 'L0_attn_Wq1': _L0_attn_in['Wq1'], 'L0_attn_Wq2': _L0_attn_in['Wq2'], 'L0_attn_Wk': _L0_attn_in['Wk'], 'L0_attn_Wv': _L0_attn_in['Wv'], 'L0_attn_Wlam': _L0_attn_in['Wlam'], 'L0_attn_Wo': _L0_attn_in['Wo'], 'L0_ffn_router_weight': _L0_ffn_in['router_weight'], 'L0_ffn_sh_gate': _L0_ffn_in['sh_gate'], 'L0_ffn_sh_up': _L0_ffn_in['sh_up'], 'L0_ffn_sh_down': _L0_ffn_in['sh_down'], 'L0_ffn_r_gate': _L0_ffn_in['r_gate'], 'L0_ffn_r_up': _L0_ffn_in['r_up'], 'L0_ffn_r_down': _L0_ffn_in['r_down']}
    _x0 = _d['L0_attn_x']
    _d['L0_attn_x'] = jax.random.normal(jax.random.fold_in(jax.random.key(seed), 1), (8, 256, 256), dtype=_x0.dtype)
    del _x0
    return _d

def reference(L0_attn_x, L0_attn_Wq1, L0_attn_Wq2, L0_attn_Wk, L0_attn_Wv, L0_attn_Wlam, L0_attn_Wo, L0_ffn_router_weight, L0_ffn_sh_gate, L0_ffn_sh_up, L0_ffn_sh_down, L0_ffn_r_gate, L0_ffn_r_up, L0_ffn_r_down):

    def _L0_attn_ref(x, Wq1, Wq2, Wk, Wv, Wlam, Wo):
        import jax, jax.numpy as jnp
        import numpy as np
        H = 16

        def _split_heads(x, h):
            B, T, D = x.shape
            return x.reshape(B, T, h, D // h).transpose(0, 2, 1, 3)
        B, T, D = x.shape
        d = D // H
        q1 = _split_heads(x @ Wq1, H)
        q2 = _split_heads(x @ Wq2, H)
        k = _split_heads(x @ Wk, H)
        v = _split_heads(x @ Wv, H)
        q = jnp.concatenate([q1, q2], axis=1)
        k2 = jnp.repeat(k, 2, axis=1)
        v2 = jnp.repeat(v, 2, axis=1)
        scale = 1.0 / jnp.sqrt(jnp.asarray(d, dtype=x.dtype))
        scores = jnp.einsum('bhqd,bhkd->bhqk', q, k2) * scale
        causal = jnp.tril(jnp.ones((T, T), dtype=bool))
        scores = jnp.where(causal, scores, jnp.finfo(scores.dtype).min)
        p = jax.nn.softmax(scores, axis=-1)
        y = jnp.einsum('bhqk,bhkd->bhqd', p, v2)
        y1, y2 = (y[:, :H], y[:, H:])
        lam = jax.nn.sigmoid(x @ Wlam).transpose(0, 2, 1)[..., None]
        y = y1 - lam * y2
        y = y.transpose(0, 2, 1, 3).reshape(B, T, D)
        return y @ Wo

    def _L0_ffn_ref(hidden_states, router_weight, sh_gate, sh_up, sh_down, r_gate, r_up, r_down):
        import jax, jax.numpy as jnp
        import numpy as np
        HIDDEN = 256
        INTER = 1024
        MOE_INTER = 128
        N_ROUTED = 8
        NUM_LOCAL = 8
        TOP_K = 2
        B, S = (4, 256)

        def _mlp(x, gw, uw, dw):
            g = x @ gw.T
            u = x @ uw.T
            return g * jax.nn.sigmoid(g) * u @ dw.T
        Bsz, Seq, H = hidden_states.shape
        x = hidden_states.reshape(-1, H)
        logits = x.astype(jnp.float32) @ router_weight.astype(jnp.float32).T
        topk_vals, topk_idx = jax.lax.top_k(logits, TOP_K)
        topk_w = jax.nn.softmax(topk_vals, axis=-1)
        slot_mask = (topk_idx < NUM_LOCAL).astype(topk_w.dtype)
        comb_w = jnp.sum(topk_w * slot_mask, axis=-1).astype(x.dtype)
        shared = _mlp(x, sh_gate, sh_up, sh_down)
        routed = _mlp(x, r_gate, r_up, r_down) * comb_w[:, None]
        return (shared + routed).reshape(Bsz, Seq, H)
    x = L0_attn_x
    x = _layernorm(x + _L0_attn_ref(x, L0_attn_Wq1, L0_attn_Wq2, L0_attn_Wk, L0_attn_Wv, L0_attn_Wlam, L0_attn_Wo), axis=-1)
    x = _layernorm(x + _L0_ffn_ref(x, L0_ffn_router_weight, L0_ffn_sh_gate, L0_ffn_sh_up, L0_ffn_sh_down, L0_ffn_r_gate, L0_ffn_r_up, L0_ffn_r_down), axis=-1)
    return x

_drawn_inputs = setup_inputs


def setup_inputs(seed=0):
    import zlib

    import numpy as np

    out = dict(_drawn_inputs(seed))
    spreads = {}
    factors = {'L0_attn_Wq1': 8.0,
     'L0_attn_Wq2': 8.0,
     'L0_attn_Wk': 8.0,
     'L0_attn_Wv': 3.24,
     'L0_attn_Wlam': 8.0,
     'L0_attn_Wo': 3.257,
     'L0_ffn_router_weight': 64.0,
     'L0_ffn_r_gate': 4.858,
     'L0_ffn_r_up': 4.773,
     'L0_ffn_r_down': 4.764,
     'L0_ffn_sh_gate': 3.593,
     'L0_ffn_sh_up': 3.556,
     'L0_ffn_sh_down': 3.549}
    for name, (base, spread) in spreads.items():
        noise = np.random.default_rng([zlib.crc32(name.encode()), seed]).standard_normal(out[name].shape)
        drawn = base * np.exp(spread * noise) if base else spread * noise
        out[name] = jnp.asarray(drawn.astype(out[name].dtype))
    for name, factor in factors.items():
        out[name] = (out[name] * factor).astype(out[name].dtype)
    return out
```

```python
from contextlib import ExitStack

import concourse.bass as bass
from concourse import mybir

P = 128
B, T, D = 8, 256, 256
HEADS = 16
HEAD_DIM = D // HEADS
QHEADS = 2 * HEADS
INTER, MOE_INTER, ROUTED = 1024, 128, 8
TT = T // P
DK = D // P
FF_UNITS = (INTER + MOE_INTER) // P
SHARED_UNITS = INTER // P
QK_BLOCKS = 3 * D // P
QK_JOBS = QK_BLOCKS // 2
BLOCK_HEADS = P // HEAD_DIM
STACK_HEADS = QHEADS + HEADS
PROJ_COLS = 4 * D + HEADS
Q_PARTS = (0, 0, 0, 1, 1, 2)
K_PARTS = (0, 1, 2, 0, 1, 0)
SLOTS = len(Q_PARTS)
STACK_ROWS = SLOTS * HEAD_DIM
MAX_PARTS = 2
GROUPS = 8
CONSTS = 5
V_COLS = 32
RING = 3
S_UNITS = QHEADS // 4 + QHEADS // 2
T_UNITS = 3 * GROUPS
FF_EARLY = 4
SCALE = float(HEAD_DIM) ** -0.5
NEG = -3.0e38
EPS = 1e-5
RSQRT_SEED = float(0x5F3759DF)

F32 = mybir.dt.float32
F32R = mybir.dt.float32r
BF16 = mybir.dt.bfloat16
I32 = mybir.dt.int32
ALU = mybir.AluOpType
ACT = mybir.ActivationFunctionType
AX_X = mybir.AxisListType.X


def build_layer(nc, x, xT, w_proj, w_out, w_gu, w_down, w_router, out):
    with ExitStack() as ctx:
        def sb(name, shape, dt=F32):
            return ctx.enter_context(nc.sbuf_tensor(name, shape, dt))

        def sem(name):
            return ctx.enter_context(nc.semaphore(name))

        scratch = nc.dram_tensor("qk_parts_dram", [3, HEAD_DIM, STACK_HEADS, T], BF16, kind="Internal").ap()

        wp_hi, wp_lo = sb("wp_hi", [P, DK, PROJ_COLS], F32R), sb("wp_lo", [P, DK, PROJ_COLS], F32R)
        wo_hi, wo_lo = sb("wo_hi", [P, DK, D], F32R), sb("wo_lo", [P, DK, D], F32R)
        wg_hi, wg_lo = sb("wg_hi", [P, DK, 2 * FF_UNITS * P], F32R), sb("wg_lo", [P, DK, 2 * FF_UNITS * P], F32R)
        wd_hi, wd_lo = sb("wd_hi", [P, FF_UNITS, D], F32R), sb("wd_lo", [P, FF_UNITS, D], F32R)
        wr_hi, wr_lo = sb("wr_hi", [P, DK, P], F32R), sb("wr_lo", [P, DK, P], F32R)
        ident = sb("ident", [P, P])
        ident_b = sb("ident_b", [P, P], BF16)
        mask_b = sb("mask_b", [P, P], BF16)
        xt_raw = sb("xt_raw", [P, DK, T])
        xt_hi, xt_lo = sb("xt_hi", [P, DK, T], F32R), sb("xt_lo", [P, DK, T], F32R)
        parts = sb("parts", [P, 3, QK_BLOCKS, T], BF16)
        rest = sb("rest", [P, QK_JOBS, 2 * T])
        q_stack = sb("q_stack", [P, QHEADS, T], BF16)
        k_stack = sb("k_stack", [P, HEADS, T], BF16)
        v_ones = sb("v_ones", [P, TT, HEADS, V_COLS])
        lam_th = sb("lam_th", [P, TT, HEADS])
        lam = sb("lam", [P, TT, HEADS])
        neg_max = sb("neg_max", [P, TT, QHEADS])
        max_parts = sb("max_parts", [QHEADS, MAX_PARTS, T], BF16)
        prob = sb("prob", [P, RING, 3, 2 * T])
        yv = sb("yv", [P, GROUPS, T])
        recip = sb("recip", [P, 3, HEADS])
        y1 = sb("y1", [P, TT, D])
        y2 = sb("y2", [P, TT, D])
        yT_hi, yT_lo = sb("yT_hi", [P, DK, T], F32R), sb("yT_lo", [P, DK, T], F32R)
        x_in = sb("x_in", [P, TT, D])
        z1 = sb("z1", [P, TT, D])
        x1 = sb("x1", [P, TT, D])
        x1_keep = sb("x1_keep", [P, TT, D])
        x1T_hi, x1T_lo = sb("x1T_hi", [P, DK, T], F32R), sb("x1T_lo", [P, DK, T], F32R)
        ln_stats = sb("ln_stats", [P, 2, TT, 6])
        ln_mv = sb("ln_mv", [P, 2, TT, 2])
        ln_t = sb("ln_t", [P, 2, 4, TT])
        ln_i = sb("ln_i", [P, 2, TT], I32)
        gate_t = sb("gate_t", [P, RING, T])
        h_full = sb("h_full", [P, RING, T])
        h_hi, h_lo = sb("h_hi", [P, FF_UNITS, T], F32R), sb("h_lo", [P, FF_UNITS, T], F32R)
        logitT = sb("logitT", [ROUTED, T])
        top8 = sb("top8", [P, TT, 8])
        comb = sb("comb", [P, 6, TT])
        z2 = sb("z2", [P, TT, D])
        out_t = sb("out_t", [P, TT, D])

        ring = [ctx.enter_context(nc.psum_tensor(f"ring{k}", [P, 512], F32)) for k in range(RING)]
        ybank = [ctx.enter_context(nc.psum_tensor(f"ybank{k}", [P, 512], F32)) for k in range(2)]
        misc = ctx.enter_context(nc.psum_tensor("misc", [P, 512], F32))
        ff = [ctx.enter_context(nc.psum_tensor(f"ff{k}", [P, 512], F32)) for k in range(2)]

        xt_loaded, x_loaded = sem("xt_loaded"), sem("x_loaded")
        wp_loaded, wo_loaded, wr_loaded = sem("wp_loaded"), sem("wo_loaded"), sem("wr_loaded")
        wg_loaded = [sem(f"wg{k}_loaded") for k in range(DK)]
        wd_loaded = sem("wd_loaded")
        parts_stored, stack_loaded, max_loaded, out_stored = sem("parts_stored"), sem("stack_loaded"), sem("max_loaded"), sem("out_stored")
        wait_passed = sem("wait_passed")
        consts_made, const_step = sem("consts_made"), sem("const_step")
        w_hi_done, w_lo_done = sem("w_hi_done"), sem("w_lo_done")
        xt_hi_done, xt_lo_done = sem("xt_hi_done"), sem("xt_lo_done")
        qk_full, qk_h_done, qk_rest_done, qk_m_done, qk_l_done = (sem(n) for n in ("qk_full", "qk_h_done", "qk_rest_done", "qk_m_done", "qk_l_done"))
        v_full, v_copied, v_done = sem("v_full"), sem("v_copied"), sem("v_done")
        s_full, max_done = sem("s_full"), sem("max_done")
        maxT_full, max_h_done, max_l_done = sem("maxT_full"), sem("max_h_done"), sem("max_l_done")
        t_full, exp_done, causal_done, pv_full, yv_done = (sem(n) for n in ("t_full", "exp_done", "causal_done", "pv_full", "yv_done"))
        y1_full, y2_full, y1_done, y2_done, y_done = (sem(n) for n in ("y1_full", "y2_full", "y1_done", "y2_done", "y_done"))
        yT_full, yT_hi_done, yT_lo_done, wo_full, z1_done = (sem(n) for n in ("yT_full", "yT_hi_done", "yT_lo_done", "wo_full", "z1_done"))
        x1_done, x1T_full, x1T_hi_done, x1T_lo_done, x1_kept = (sem(n) for n in ("x1_done", "x1T_full", "x1T_hi_done", "x1T_lo_done", "x1_kept"))
        attn_step = sem("attn_step")
        gu_full, gate_th_done, gate_done, h_done, h_hi_done, h_lo_done = (sem(n) for n in ("gu_full", "gate_th_done", "gate_done", "h_done", "h_hi_done", "h_lo_done"))
        logitT_full, logitT_done, logit_full, top_done, top_exp_done = (sem(n) for n in ("logitT_full", "logitT_done", "logit_full", "top_done", "top_exp_done"))
        shared_full, routed_full, z2_shared_done, z2_done, out_done = (sem(n) for n in ("shared_full", "routed_full", "z2_shared_done", "z2_done", "out_done"))
        mlp_step = sem("mlp_step")
        ATTN_STEPS = 1 + 3 * TT + LN_STEPS
        MLP_STEPS = 5 + LN_STEPS

        def own_wait(eng):
            eng.sem_inc(wait_passed, 1)

        block = ctx.enter_context(nc.Block())

        @block.sync
        def _(sp):
            def load_xt(b):
                if not isinstance(b, int) or b > 0:
                    sp.wait_ge(xt_hi_done, b)
                    sp.wait_ge(xt_lo_done, b)
                    own_wait(sp)
                sp.dma_start(xt_raw[:, :, :], xT[b].rearrange("(k p) t -> p k t", p=P)).then_inc(xt_loaded, 16)

            def store_parts(b):
                for n in range(QK_JOBS):
                    for p, made in enumerate((qk_h_done, qk_m_done, qk_l_done)):
                        sp.wait_ge(made, b * QK_JOBS + n + 1)
                        for blk in (2 * n, 2 * n + 1):
                            sp.dma_start(scratch[p].rearrange("d (b r) t -> r d b t", r=BLOCK_HEADS)[:, :, blk, :],
                                         parts[:, p, blk, :]).then_inc(parts_stored, 16)

            def load_stacks(b):
                sp.wait_ge(parts_stored, (b + 1) * (16 * 3 * QK_BLOCKS))
                own_wait(sp)
                if not isinstance(b, int) or b > 0:
                    sp.wait_ge(t_full, b * T_UNITS)
                for s in range(SLOTS):
                    rows = slice(HEAD_DIM * s, HEAD_DIM * (s + 1))
                    sp.dma_start(q_stack[rows, :, :], scratch[Q_PARTS[s], :, 0:QHEADS, :]).then_inc(stack_loaded, 16)
                    sp.dma_start(k_stack[rows, :, :], scratch[K_PARTS[s], :, QHEADS:STACK_HEADS, :]).then_inc(stack_loaded, 16)

            def load_max(b):
                for p, made in enumerate((max_h_done, max_l_done)):
                    sp.wait_ge(made, b + 1)
                    sp.dma_start(q_stack[STACK_ROWS + p:STACK_ROWS + p + 1, :, :], max_parts[:, p, :]).then_inc(max_loaded, 16)

            def load_x(b):
                if not isinstance(b, int) or b > 0:
                    sp.wait_ge(z1_done, b)
                    own_wait(sp)
                sp.dma_start(x_in[:, :, :], x[b].rearrange("(t p) d -> p t d", p=P)).then_inc(x_loaded, 16)

            def store_out(b):
                sp.wait_ge(out_done, (b + 1) * TT)
                own_wait(sp)
                sp.dma_start(out[b].rearrange("(t p) d -> p t d", p=P), out_t[:, :, :]).then_inc(out_stored, 16)

            def iteration(i, has_next, has_prev):
                if has_next:
                    load_xt(i + 1)
                load_x(i)
                if has_next:
                    store_parts(i + 1)
                load_max(i)
                if has_next:
                    load_stacks(i + 1)
                if has_prev:
                    store_out(i - 1)

            sp.sem_inc(out_stored, 16)
            load_xt(0)
            stage = prob[:, :, :, :].rearrange("p a b c -> p (a b c)")
            cols = DK * PROJ_COLS
            sp.dma_start(stage[:, 0:cols].rearrange("p (k n) -> p k n", k=DK),
                         w_proj.rearrange("(k p) n -> p k n", p=P)).then_inc(wp_loaded, 16)
            sp.dma_start(z1[:, :, :], w_out.rearrange("(k p) n -> p k n", p=P)).then_inc(wo_loaded, 16)
            sp.wait_ge(consts_made, 1)
            sp.dma_start(z2[:, :, 0:ROUTED], w_router.rearrange("(k p) n -> p k n", p=P)).then_inc(wr_loaded, 16)
            half = 2 * FF_UNITS * P
            sp.dma_start(stage[:, half:2 * half], w_gu[P:2 * P, :]).then_inc(wg_loaded[1], 16)
            sp.wait_ge(w_hi_done, 1)
            sp.wait_ge(w_lo_done, 1)
            sp.dma_start(stage[:, 0:half], w_gu[0:P, :]).then_inc(wg_loaded[0], 16)
            store_parts(0)
            load_stacks(0)
            sp.wait_ge(w_hi_done, 4)
            sp.wait_ge(w_lo_done, 4)
            sp.dma_start(stage[:, half:2 * half].rearrange("p (n d) -> p n d", d=D),
                         w_down.rearrange("(n p) d -> p n d", p=P)).then_inc(wd_loaded, 16)
            iteration(0, True, False)
            with sp.Fori(1, B - 1) as i:
                iteration(i, True, True)
            iteration(B - 1, False, True)
            store_out(B - 1)
            sp.wait_ge(out_stored, 16 * (B + 1))

        @block.gpsimd
        def _(pool):
            pool.memset(k_stack[STACK_ROWS:STACK_ROWS + MAX_PARTS, :, :], 1.0).then_inc(const_step, 1)
            pool.wait_ge(const_step, 1)
            pool.memset(z2[:, :, :], 0.0).then_inc(consts_made, 1)
            pool.memset(ident[:, :], 0.0).then_inc(const_step, 1)
            pool.memset(ident_b[:, :], 0.0).then_inc(const_step, 1)
            pool.memset(mask_b[:, :], 0.0).then_inc(const_step, 1)
            pool.memset(v_ones[:, :, :, HEAD_DIM:V_COLS], 0.0).then_inc(const_step, 1)
            pool.wait_ge(const_step, 5)
            for m in (ident, ident_b):
                pool.affine_select(out=m[:, :], in_=m[:, :], compare_op=ALU.not_equal, fill=1.0, base=0,
                                   pattern=[[-1, P]], channel_multiplier=1).then_inc(consts_made, 1)
            pool.affine_select(out=mask_b[:, :], in_=mask_b[:, :], compare_op=ALU.is_ge, fill=NEG, base=0,
                               pattern=[[-1, P]], channel_multiplier=1).then_inc(consts_made, 1)
            pool.memset(v_ones[:, :, :, HEAD_DIM:HEAD_DIM + 1], 1.0).then_inc(consts_made, 1)

            def third_parts(b):
                if not isinstance(b, int) or b > 0:
                    pool.wait_ge(parts_stored, b * (16 * 3 * QK_BLOCKS))
                for n in range(QK_JOBS):
                    pool.wait_ge(qk_m_done, b * QK_JOBS + n + 1)
                    view = "p (b t) -> p b t"
                    pool.tensor_tensor(parts[:, 2, 2 * n:2 * n + 2, :], rest[:, n, :].rearrange(view, b=2),
                                       parts[:, 1, 2 * n:2 * n + 2, :], ALU.subtract).then_inc(qk_l_done, 1)

            def h_rests(b, units):
                for n in units:
                    pool.wait_ge(h_hi_done, b * FF_UNITS + n + 1)
                    pool.tensor_tensor(h_lo[:, n, :], h_full[:, n % RING, :], h_hi[:, n, :].bitcast(F32),
                                       ALU.subtract).then_inc(h_lo_done, 1)

            def causal(b):
                for g in range(GROUPS):
                    first = prob[:, g % RING, 0:2, :].rearrange("p x (h q) -> p (x h) q", h=2)[:, :, 0:P]
                    last = prob[:, g % RING, 2, :].rearrange("p (h q) -> p h q", q=P)
                    for units, v in ((2, first), (3, last)):
                        pool.wait_ge(exp_done, b * T_UNITS + 3 * g + units)
                        own_wait(pool)
                        pool.affine_select(out=v, in_=v, compare_op=ALU.is_ge, fill=0.0, base=0,
                                           pattern=[[0, 4], [1, P]], channel_multiplier=-1).then_inc(causal_done, 1)

            def iteration(i, has_next, has_prev):
                if has_next:
                    third_parts(i + 1)
                if has_prev:
                    h_rests(i - 1, range(FF_EARLY))
                causal(i)
                if has_prev:
                    h_rests(i - 1, range(FF_EARLY, FF_UNITS))

            third_parts(0)
            iteration(0, True, False)
            with pool.Fori(1, B - 1) as i:
                iteration(i, True, True)
            iteration(B - 1, False, True)
            h_rests(B - 1, range(FF_UNITS))

        @block.scalar
        def _(act):
            def copy(o, i):
                return nc.scalar.activation(o, i, ACT.Copy)

            def split_xt(b):
                act.wait_ge(xt_loaded, (b + 1) * 16)
                copy(xt_hi[:, :, :], xt_raw[:, :, :]).then_inc(xt_hi_done, 1)

            def first_part(b, n):
                act.wait_ge(qk_full, b * QK_JOBS + n + 1)
                copy(parts[:, 0, 2 * n:2 * n + 2, :], misc[:, :].rearrange("p (b t) -> p b t", b=2)).then_inc(qk_h_done, 1)

            def values(b):
                for t in range(TT):
                    act.wait_ge(v_full, b * TT + t + 1)
                    copy(v_ones[:, t, :, 0:HEAD_DIM], misc[:, 0:D].rearrange("p (h d) -> p h d", h=HEADS)).then_inc(v_copied, 1)
                    act.activation(lam_th[:, t, :], misc[:, D:D + HEADS], ACT.Tanh, scale=0.5).then_inc(v_done, 1)

            def max_first(b):
                act.wait_ge(maxT_full, b + 1)
                if not isinstance(b, int) or b > 0:
                    act.wait_ge(max_loaded, b * (16 * MAX_PARTS))
                copy(max_parts[:, 0, :], misc[0:QHEADS, 0:T]).then_inc(max_h_done, 1)

            def exps(b):
                for g in range(GROUPS):
                    for u in range(3):
                        act.wait_ge(t_full, b * T_UNITS + 3 * g + u + 1)
                        if u == 0 and g >= RING:
                            act.wait_ge(pv_full, b * GROUPS + g - RING + 1)
                        act.activation(prob[:, g % RING, u, :], ring[u][:, :], ACT.Exp, scale=SCALE).then_inc(exp_done, 1)

            def gate_tanh(b, n):
                act.wait_ge(gu_full, b * FF_UNITS + n + 1)
                if n >= RING:
                    act.wait_ge(h_done, b * FF_UNITS + n - RING + 1)
                act.activation(gate_t[:, n % RING, :], ff[n % 2][:, 0:T], ACT.Tanh, scale=0.5).then_inc(gate_th_done, 1)

            def h_first(b, n):
                act.wait_ge(h_done, b * FF_UNITS + n + 1)
                copy(h_hi[:, n, :], h_full[:, n % RING, :]).then_inc(h_hi_done, 1)

            def mlp_units(b, units):
                for n in units:
                    gate_tanh(b, n)
                    if n > units[0]:
                        h_first(b, n - 1)
                h_first(b, units[-1])

            def yT_first(b):
                act.wait_ge(yT_full, b + 1)
                copy(yT_hi[:, :, :], misc[:, :].rearrange("p (k t) -> p k t", k=DK)).then_inc(yT_hi_done, 1)

            def x1T_first(b, has_prev):
                if has_prev:
                    act.wait_ge(z2_shared_done, b)
                act.wait_ge(x1_done, (b + 1) * TT)
                copy(x1_keep[:, :, :], x1[:, :, :]).then_inc(x1_kept, 1)
                act.wait_ge(x1T_full, b + 1)
                copy(x1T_hi[:, :, :], misc[:, :].rearrange("p (k t) -> p k t", k=DK)).then_inc(x1T_hi_done, 1)

            def router(b):
                act.wait_ge(logitT_full, b + 1)
                copy(logitT[:, :], ff[1][0:ROUTED, 0:T]).then_inc(logitT_done, 1)

            def router_exp(b):
                act.wait_ge(mlp_step, b * MLP_STEPS + 1)
                act.activation(comb[:, 1, :], comb[:, 0, :], ACT.Exp).then_inc(top_exp_done, 1)

            def iteration(i, has_next, has_prev):
                if has_next:
                    split_xt(i + 1)
                    act.wait_ge(parts_stored, (i + 1) * (16 * 3 * QK_BLOCKS))
                    for n in range(QK_JOBS):
                        first_part(i + 1, n)
                max_first(i)
                if has_prev:
                    mlp_units(i - 1, range(FF_EARLY))
                exps(i)
                if has_prev:
                    mlp_units(i - 1, range(FF_EARLY, FF_UNITS))
                    router(i - 1)
                    router_exp(i - 1)
                yT_first(i)
                x1T_first(i, has_prev)
                if has_next:
                    values(i + 1)

            def split_weight(hi, raw, loaded):
                act.wait_ge(loaded, 16)
                copy(hi, raw).then_inc(w_hi_done, 1)

            stage = prob[:, :, :, :].rearrange("p a b c -> p (a b c)")
            half = 2 * FF_UNITS * P
            split_xt(0)
            split_weight(wp_hi[:, :, :], stage[:, 0:DK * PROJ_COLS].rearrange("p (k n) -> p k n", k=DK), wp_loaded)
            for n in range(QK_JOBS):
                first_part(0, n)
            act.wait_ge(consts_made, CONSTS)
            values(0)
            split_weight(wo_hi[:, :, :], z1[:, :, :], wo_loaded)
            split_weight(wr_hi[:, :, :], z2[:, :, 0:P], wr_loaded)
            split_weight(wg_hi[:, 1, :], stage[:, half:2 * half], wg_loaded[1])
            split_weight(wg_hi[:, 0, :], stage[:, 0:half], wg_loaded[0])
            split_weight(wd_hi[:, :, :], stage[:, half:2 * half].rearrange("p (n d) -> p n d", d=D), wd_loaded)
            act.wait_ge(w_lo_done, 6)
            iteration(0, True, False)
            with act.Fori(1, B - 1) as i:
                iteration(i, True, True)
            iteration(B - 1, False, True)
            mlp_units(B - 1, range(FF_UNITS))
            router(B - 1)
            router_exp(B - 1)

        @block.tensor
        def _(pe):
            def product(o, lhs_hi, lhs_lo, rhs_hi, rhs_lo, first, last):
                pe.matmul(o, lhs_lo, rhs_hi, start=first, stop=False)
                pe.matmul(o, lhs_hi, rhs_lo, start=False, stop=False)
                return pe.matmul(o, lhs_hi, rhs_hi, start=False, stop=last)

            def qk_job(b, n):
                if n == 0:
                    pe.wait_ge(xt_hi_done, b + 1)
                    pe.wait_ge(xt_lo_done, b + 1)
                    if not isinstance(b, int) or b > 0:
                        pe.wait_ge(v_done, b * TT)
                else:
                    pe.wait_ge(qk_rest_done, b * QK_JOBS + n)
                for h in range(2):
                    f = slice((2 * n + h) * P, (2 * n + h + 1) * P)
                    for k in range(DK):
                        mm = product(misc[:, h * T:(h + 1) * T], wp_hi[:, k, f], wp_lo[:, k, f],
                                     xt_hi[:, k, :], xt_lo[:, k, :], k == 0, k == DK - 1)
                mm.then_inc(qk_full, 1)

            def v_job(b, t):
                if t == 0:
                    if isinstance(b, int) and b == 0:
                        pe.wait_ge(qk_rest_done, QK_JOBS)
                    else:
                        pe.wait_ge(x1T_lo_done, b)
                else:
                    pe.wait_ge(v_done, b * TT + t)
                q = slice(t * P, (t + 1) * P)
                w = slice(3 * D, PROJ_COLS)
                for k in range(DK):
                    mm = product(misc[:, 0:D + HEADS], xt_hi[:, k, q], xt_lo[:, k, q], wp_hi[:, k, w], wp_lo[:, k, w],
                                 k == 0, k == DK - 1)
                mm.then_inc(v_full, 1)

            def s_unit(b, u):
                if u < RING:
                    if not isinstance(b, int) or b > 0:
                        pe.wait_ge(exp_done, b * T_UNITS - RING + u + 1)
                else:
                    pe.wait_ge(max_done, b * S_UNITS + u - RING + 1)
                bank = ring[u % RING]
                if u < QHEADS // 4:
                    t, heads, keys = 0, range(4 * u, 4 * u + 4), P
                else:
                    n = u - QHEADS // 4
                    t, heads, keys = 1, range(2 * n, 2 * n + 2), T
                o = bank[:, :].rearrange("p (h k) -> p h k", k=keys)
                pe.matmul(o[:, :, keys - P:keys], ident_b[:, :], mask_b[:, :].unsqueeze(1).to_broadcast([P, len(heads), P]),
                          start=True, stop=False, skip_group_check=True)
                for j, h in enumerate(heads):
                    mm = pe.matmul(o[:, j, :], q_stack[0:STACK_ROWS, h, t * P:(t + 1) * P], k_stack[0:STACK_ROWS, h // 2, 0:keys],
                                   start=False, stop=True, skip_group_check=True)
                mm.then_inc(s_full, 1)

            def max_job(b, has_next):
                pe.wait_ge(max_done, b * S_UNITS + S_UNITS)
                if has_next:
                    pe.wait_ge(qk_rest_done, (b + 2) * QK_JOBS)
                else:
                    pe.wait_ge(v_done, (b + 1) * TT)
                for t in range(TT):
                    mm = pe.transpose(misc[0:QHEADS, t * P:(t + 1) * P], neg_max[:, t, :], ident[:, :])
                mm.then_inc(maxT_full, 1)

            def t_group(b, g):
                rows = slice(0, STACK_ROWS + MAX_PARTS)
                for u in range(3):
                    if g == 0:
                        pe.wait_ge(max_done, b * S_UNITS + S_UNITS - RING + u + 1)
                    else:
                        pe.wait_ge(exp_done, b * T_UNITS + 3 * (g - 1) + u + 1)
                    if u < 2:
                        n = 2 * g + u
                        mm = pe.matmul(ring[u][:, :].rearrange("p (h q) -> p h q", h=2), k_stack[rows, n, 0:P],
                                       q_stack[rows, 2 * n:2 * n + 2, :], start=True, stop=True)
                    else:
                        for j in range(2):
                            n = 2 * g + j
                            mm = pe.matmul(ring[u][:, j * T:(j + 1) * T].rearrange("p (h q) -> p h q", h=2), k_stack[rows, n, P:T],
                                           q_stack[rows, 2 * n:2 * n + 2, P:T], start=True, stop=True)
                    mm.then_inc(t_full, 1)

            def pv_group(b, g):
                bank = ybank[g % 2]
                if g >= 2:
                    pe.wait_ge(yv_done, b * GROUPS + g - 1)
                elif not isinstance(b, int) or b > 0:
                    if g == 0:
                        pe.wait_ge(z1_done, b)
                    else:
                        pe.wait_ge(y2_done, b * TT)
                for t in range(TT):
                    pe.wait_ge(causal_done, b * (2 * GROUPS) + 2 * g + t + 1)
                    for j in range(4):
                        if t == 0:
                            p = prob[:, g % RING, j // 2, (j % 2) * T:(j % 2 + 1) * T]
                        else:
                            p = prob[:, g % RING, 2, j * P:(j + 1) * P]
                        mm = pe.matmul(bank[V_COLS * j:V_COLS * (j + 1), t * P:T], v_ones[:, t, 2 * g + j // 2, :], p,
                                       start=(t == 0), stop=(t == TT - 1))
                mm.then_inc(pv_full, 1)

            def y_jobs(b, t):
                for k, (done, full) in enumerate(((y1_done, y1_full), (y2_done, y2_full))):
                    if t == 0:
                        pe.wait_ge(yv_done, b * GROUPS + (k + 1) * (GROUPS // 2))
                        pe.wait_ge(yv_done, b * GROUPS + GROUPS - 1 + k)
                    else:
                        pe.wait_ge(done, b * TT + t)
                    for j in range(4):
                        mm = pe.transpose(ybank[k][:, j * P:(j + 1) * P], yv[:, 4 * k + j, t * P:(t + 1) * P], ident[:, :])
                    mm.then_inc(full, 1)

            def yT_job(b):
                pe.wait_ge(max_l_done, b + 1)
                for t in range(TT):
                    pe.wait_ge(y_done, b * TT + t + 1)
                    for k in range(DK):
                        mm = pe.transpose(misc[:, k * T + t * P:k * T + (t + 1) * P], y1[:, t, k * P:(k + 1) * P], ident[:, :])
                mm.then_inc(yT_full, 1)

            def wo_job(b):
                pe.wait_ge(yT_hi_done, b + 1)
                pe.wait_ge(yT_lo_done, b + 1)
                pe.wait_ge(y1_done, (b + 1) * TT)
                for t in range(TT):
                    q = slice(t * P, (t + 1) * P)
                    for k in range(DK):
                        mm = product(ybank[0][:, t * D:(t + 1) * D], yT_hi[:, k, q], yT_lo[:, k, q], wo_hi[:, k, :], wo_lo[:, k, :],
                                     k == 0, k == DK - 1)
                mm.then_inc(wo_full, 1)

            def x1T_job(b):
                pe.wait_ge(yT_lo_done, b + 1)
                for t in range(TT):
                    pe.wait_ge(x1_done, b * TT + t + 1)
                    for k in range(DK):
                        mm = pe.transpose(misc[:, k * T + t * P:k * T + (t + 1) * P], x1[:, t, k * P:(k + 1) * P], ident[:, :])
                mm.then_inc(x1T_full, 1)

            def gu_units(b, units):
                for n in units:
                    if n == 0:
                        pe.wait_ge(x1T_hi_done, b + 1)
                        pe.wait_ge(x1T_lo_done, b + 1)
                    if n < 2:
                        pe.wait_ge(z2_done, (b + 1) * TT)
                    else:
                        pe.wait_ge(h_done, b * FF_UNITS + n - 1)
                    for j in range(2):
                        f = slice((2 * n + j) * P, (2 * n + j + 1) * P)
                        for k in range(DK):
                            mm = product(ff[n % 2][:, j * T:(j + 1) * T], wg_hi[:, k, f], wg_lo[:, k, f], x1T_hi[:, k, :], x1T_lo[:, k, :],
                                         k == 0, k == DK - 1)
                    mm.then_inc(gu_full, 1)

            def router_jobs(b):
                pe.wait_ge(h_done, b * FF_UNITS + FF_UNITS - 1)
                for k in range(DK):
                    mm = product(ff[1][:, 0:T], wr_hi[:, k, :], wr_lo[:, k, :], x1T_hi[:, k, :], x1T_lo[:, k, :], k == 0, k == DK - 1)
                mm.then_inc(logitT_full, 1)

            def logit_job(b):
                pe.wait_ge(logitT_done, b + 1)
                pe.wait_ge(h_done, b * FF_UNITS + FF_UNITS)
                own_wait(pe)
                for t in range(TT):
                    mm = pe.transpose(ff[0][:, t * ROUTED:(t + 1) * ROUTED], logitT[:, t * P:(t + 1) * P], ident[0:ROUTED, 0:ROUTED])
                mm.then_inc(logit_full, 1)

            def down_job(b, bank, units, full):
                for t in range(TT):
                    q = slice(t * P, (t + 1) * P)
                    for n in units:
                        if t == 0:
                            pe.wait_ge(h_lo_done, b * FF_UNITS + n + 1)
                        mm = product(bank[:, t * D:(t + 1) * D], h_hi[:, n, q], h_lo[:, n, q], wd_hi[:, n, :], wd_lo[:, n, :],
                                     n == units[0], n == units[-1])
                mm.then_inc(full, 1)

            def shared_job(b):
                pe.wait_ge(logitT_done, b + 1)
                down_job(b, ff[1], range(SHARED_UNITS), shared_full)

            def routed_job(b):
                pe.wait_ge(top_done, (b + 1) * TT)
                down_job(b, ff[0], range(SHARED_UNITS, FF_UNITS), routed_full)

            def iteration(i, has_next, has_prev):
                pe.wait_ge(stack_loaded, (i + 1) * (16 * 2 * SLOTS))
                for u in range(S_UNITS):
                    s_unit(i, u)
                    if has_next and u in (8, 14, 20):
                        qk_job(i + 1, (u - 8) // 6)
                max_job(i, has_next)
                if has_prev:
                    gu_units(i - 1, range(FF_EARLY))
                pe.wait_ge(max_loaded, (i + 1) * (16 * MAX_PARTS))
                for g in range(GROUPS + 2):
                    if g < GROUPS:
                        t_group(i, g)
                    if g >= 2:
                        pv_group(i, g - 2)
                y_jobs(i, 0)
                y_jobs(i, 1)
                if has_prev:
                    gu_units(i - 1, range(FF_EARLY, FF_UNITS))
                    router_jobs(i - 1)
                    logit_job(i - 1)
                yT_job(i)
                if has_prev:
                    shared_job(i - 1)
                wo_job(i)
                if has_prev:
                    routed_job(i - 1)
                x1T_job(i)
                if has_next:
                    for t in range(TT):
                        v_job(i + 1, t)

            pe.wait_ge(w_hi_done, 1)
            pe.wait_ge(w_lo_done, 1)
            for n in range(QK_JOBS):
                qk_job(0, n)
            for t in range(TT):
                v_job(0, t)
            pe.wait_ge(consts_made, CONSTS)
            pe.wait_ge(w_hi_done, 6)
            pe.wait_ge(w_lo_done, 6)
            iteration(0, True, False)
            with pe.Fori(1, B - 1) as i:
                iteration(i, True, True)
            iteration(B - 1, False, True)
            gu_units(B - 1, range(FF_UNITS))
            router_jobs(B - 1)
            logit_job(B - 1)
            shared_job(B - 1)
            routed_job(B - 1)

        @block.vector
        def _(dve):
            def stepper(semaphore, done):
                count = [done]

                def step(ins):
                    count[0] = count[0] + 1
                    ins.then_inc(semaphore, 1)

                def settle():
                    dve.wait_ge(semaphore, count[0])
                return step, settle

            def layer_norm(which, z, y, y_sem, step, settle):
                stats, mv, s, seed = ln_stats[:, which], ln_mv[:, which], ln_t[:, which], ln_i[:, which, :]
                for t in range(TT):
                    step(dve.bn_stats(stats[:, t, :], z[:, t, :]))
                settle()
                own_wait(dve)
                for t in range(TT):
                    step(dve.bn_aggr(mv[:, t, :], stats[:, t, :]))
                settle()
                var, r, a = s[:, 0, :], s[:, 1, :], s[:, 2, :]
                step(dve.tensor_scalar(var, mv[:, :, 1], EPS, None, ALU.add))
                settle()
                step(dve.tensor_scalar(seed, var.bitcast(I32), 1, None, ALU.logical_shift_right))
                settle()
                step(dve.tensor_scalar(r.bitcast(I32), seed, -1.0, RSQRT_SEED, ALU.mult, ALU.add))
                settle()
                for _ in range(NEWTON):
                    step(dve.tensor_tensor(a, r, r, ALU.mult))
                    settle()
                    step(dve.scalar_tensor_tensor(a, a, -0.5, var, ALU.mult, ALU.mult))
                    settle()
                    step(dve.scalar_tensor_tensor(r, a, 1.5, r, ALU.add, ALU.mult))
                    settle()
                for t in range(TT):
                    dve.tensor_scalar(y[:, t, :], z[:, t, :], mv[:, t, 0:1], s[:, 1, t:t + 1], ALU.subtract,
                                      ALU.mult).then_inc(y_sem, 1)

            def split_xt(b):
                dve.wait_ge(xt_hi_done, b + 1)
                dve.tensor_tensor(xt_lo[:, :, :], xt_raw[:, :, :], xt_hi[:, :, :].bitcast(F32), ALU.subtract).then_inc(xt_lo_done, 1)

            def qk_rest(b, n):
                dve.wait_ge(qk_h_done, b * QK_JOBS + n + 1)
                dve.tensor_tensor(rest[:, n, :].rearrange("p (b t) -> p b t", b=2), misc[:, :].rearrange("p (b t) -> p b t", b=2),
                                  parts[:, 0, 2 * n:2 * n + 2, :], ALU.subtract).then_inc(qk_rest_done, 1)

            def qk_second(b, n):
                dve.wait_ge(qk_rest_done, b * QK_JOBS + n + 1)
                dve.tensor_copy(parts[:, 1, 2 * n:2 * n + 2, :], rest[:, n, :].rearrange("p (b t) -> p b t", b=2)).then_inc(qk_m_done, 1)

            def row_max(b, u):
                dve.wait_ge(s_full, b * S_UNITS + u + 1)
                if u < QHEADS // 4:
                    o, keys = neg_max[:, 0, 4 * u:4 * u + 4], P
                else:
                    n = u - QHEADS // 4
                    o, keys = neg_max[:, 1, 2 * n:2 * n + 2], T
                dve.tensor_reduce(o, ring[u % RING][:, :].rearrange("p (h k) -> p h k", k=keys), AX_X, ALU.max,
                                  negate=True).then_inc(max_done, 1)

            def max_second(b):
                dve.wait_ge(max_h_done, b + 1)
                dve.tensor_tensor(max_parts[:, 1, :], misc[0:QHEADS, 0:T], max_parts[:, 0, :], ALU.subtract).then_inc(max_l_done, 1)

            def mlp_units(b, units):
                for n in units:
                    dve.wait_ge(gate_th_done, b * FF_UNITS + n + 1)
                    dve.scalar_tensor_tensor(gate_t[:, n % RING, :], gate_t[:, n % RING, :], 1.0, ff[n % 2][:, 0:T], ALU.add,
                                             ALU.mult).then_inc(gate_done, 1)
                    dve.wait_ge(gate_done, b * FF_UNITS + n + 1)
                    if n >= RING:
                        dve.wait_ge(h_lo_done, b * FF_UNITS + n - RING + 1)
                    dve.scalar_tensor_tensor(h_full[:, n % RING, :], gate_t[:, n % RING, :], 0.5, ff[n % 2][:, T:2 * T], ALU.mult,
                                             ALU.mult).then_inc(h_done, 1)

            def evacuate_pv(b):
                for g in range(GROUPS):
                    dve.wait_ge(pv_full, b * GROUPS + g + 1)
                    dve.tensor_copy(yv[:, g, :], ybank[g % 2][:, 0:T]).then_inc(yv_done, 1)

            def normalize_y(b, t, step, settle):
                def heads(bank):
                    return bank[:, :].rearrange("p (h c) -> p h c", c=V_COLS)

                def wide(r):
                    return r.unsqueeze(2).to_broadcast([P, HEADS, HEAD_DIM])

                dve.wait_ge(y1_full, b * TT + t + 1)
                step(dve.reciprocal(recip[:, 0, :], heads(ybank[0])[:, :, HEAD_DIM]))
                dve.wait_ge(y2_full, b * TT + t + 1)
                step(dve.reciprocal(recip[:, 1, :], heads(ybank[1])[:, :, HEAD_DIM]))
                settle()
                step(dve.tensor_tensor(recip[:, 2, :], recip[:, 1, :], lam[:, t, :], ALU.mult))
                view = "p (h d) -> p h d"
                dve.tensor_tensor(y1[:, t, :].rearrange(view, h=HEADS), heads(ybank[0])[:, :, 0:HEAD_DIM], wide(recip[:, 0, :]),
                                  ALU.mult).then_inc(y1_done, 1)
                settle()
                dve.tensor_tensor(y2[:, t, :].rearrange(view, h=HEADS), heads(ybank[1])[:, :, 0:HEAD_DIM], wide(recip[:, 2, :]),
                                  ALU.mult).then_inc(y2_done, 1)
                dve.wait_ge(y1_done, b * TT + t + 1)
                dve.wait_ge(y2_done, b * TT + t + 1)
                dve.tensor_tensor(y1[:, t, :], y1[:, t, :], y2[:, t, :], ALU.subtract).then_inc(y_done, 1)

            def yT_second(b):
                dve.wait_ge(yT_hi_done, b + 1)
                dve.tensor_tensor(yT_lo[:, :, :], misc[:, :].rearrange("p (k t) -> p k t", k=DK), yT_hi[:, :, :].bitcast(F32),
                                  ALU.subtract).then_inc(yT_lo_done, 1)

            def first_norm(b, step, settle):
                dve.wait_ge(wo_full, b + 1)
                dve.wait_ge(x_loaded, (b + 1) * 16)
                dve.tensor_tensor(z1[:, :, :], ybank[0][:, :].rearrange("p (t d) -> p t d", t=TT), x_in[:, :, :], ALU.add).then_inc(z1_done, 1)
                dve.wait_ge(z1_done, b + 1)
                if not isinstance(b, int) or b > 0:
                    dve.wait_ge(x1_kept, b)
                layer_norm(0, z1, x1, x1_done, step, settle)

            def x1T_second(b):
                dve.wait_ge(x1T_hi_done, b + 1)
                dve.tensor_tensor(x1T_lo[:, :, :], misc[:, :].rearrange("p (k t) -> p k t", k=DK), x1T_hi[:, :, :].bitcast(F32),
                                  ALU.subtract).then_inc(x1T_lo_done, 1)

            def router(b, step, settle):
                dve.wait_ge(logit_full, b + 1)
                own_wait(dve)
                for t in range(TT):
                    dve.max(top8[:, t, :], ff[0][:, t * ROUTED:(t + 1) * ROUTED]).then_inc(top_done, 1)
                dve.wait_ge(top_done, (b + 1) * TT)
                step(dve.tensor_tensor(comb[:, 0, :], top8[:, :, 1], top8[:, :, 0], ALU.subtract))
                dve.wait_ge(top_exp_done, b + 1)
                step(dve.tensor_scalar(comb[:, 2, :], comb[:, 1, :], 1.0, None, ALU.add))
                settle()
                step(dve.reciprocal(comb[:, 3, :], comb[:, 2, :]))
                settle()
                step(dve.tensor_tensor(comb[:, 4, :], comb[:, 1, :], comb[:, 3, :], ALU.mult))
                settle()
                step(dve.tensor_tensor(comb[:, 5, :], comb[:, 3, :], comb[:, 4, :], ALU.add))

            def add_shared(b):
                dve.wait_ge(shared_full, b + 1)
                dve.wait_ge(x1_kept, b + 1)
                dve.tensor_tensor(z2[:, :, :], ff[1][:, :].rearrange("p (t d) -> p t d", t=TT), x1_keep[:, :, :], ALU.add).then_inc(z2_shared_done, 1)

            def second_norm(b, step, settle):
                dve.wait_ge(routed_full, b + 1)
                dve.wait_ge(z2_shared_done, b + 1)
                settle()
                for t in range(TT):
                    dve.scalar_tensor_tensor(z2[:, t, :], ff[0][:, t * D:(t + 1) * D], comb[:, 5, t:t + 1], z2[:, t, :], ALU.mult,
                                             ALU.add).then_inc(z2_done, 1)
                dve.wait_ge(z2_done, (b + 2) * TT)
                dve.wait_ge(out_stored, (b + 1) * 16)
                layer_norm(1, z2, out_t, out_done, step, settle)

            def iteration(i, has_next, has_prev):
                attn = stepper(attn_step, i * ATTN_STEPS)
                mlp = stepper(mlp_step, (i - 1) * MLP_STEPS)
                if has_next:
                    split_xt(i + 1)
                    dve.wait_ge(parts_stored, (i + 1) * (16 * 3 * QK_BLOCKS))
                for u in range(S_UNITS):
                    row_max(i, u)
                    if has_next and u in (8, 14, 20):
                        qk_rest(i + 1, (u - 8) // 6)
                    if has_next and u in (9, 15, 21):
                        qk_second(i + 1, (u - 9) // 6)
                max_second(i)
                attn[0](dve.tensor_scalar(lam[:, :, :], lam_th[:, :, :], 0.5, 0.5, ALU.mult, ALU.add))
                if has_prev:
                    mlp_units(i - 1, range(FF_EARLY))
                evacuate_pv(i)
                normalize_y(i, 0, *attn)
                normalize_y(i, 1, *attn)
                if has_prev:
                    mlp_units(i - 1, range(FF_EARLY, FF_UNITS))
                    router(i - 1, *mlp)
                yT_second(i)
                if has_prev:
                    add_shared(i - 1)
                first_norm(i, *attn)
                x1T_second(i)
                if has_prev:
                    second_norm(i - 1, *mlp)

            def split_weight(n, lo, raw, hi):
                dve.wait_ge(w_hi_done, n)
                dve.tensor_tensor(lo, raw, hi.bitcast(F32), ALU.subtract).then_inc(w_lo_done, 1)

            stage = prob[:, :, :, :].rearrange("p a b c -> p (a b c)")
            half = 2 * FF_UNITS * P
            dve.sem_inc(z2_done, TT)
            split_xt(0)
            split_weight(1, wp_lo[:, :, :], stage[:, 0:DK * PROJ_COLS].rearrange("p (k n) -> p k n", k=DK), wp_hi[:, :, :])
            for n in range(QK_JOBS):
                qk_rest(0, n)
                qk_second(0, n)
            split_weight(2, wo_lo[:, :, :], z1[:, :, :], wo_hi[:, :, :])
            split_weight(3, wr_lo[:, :, :], z2[:, :, 0:P], wr_hi[:, :, :])
            split_weight(4, wg_lo[:, 1, :], stage[:, half:2 * half], wg_hi[:, 1, :])
            split_weight(5, wg_lo[:, 0, :], stage[:, 0:half], wg_hi[:, 0, :])
            split_weight(6, wd_lo[:, :, :], stage[:, half:2 * half].rearrange("p (n d) -> p n d", d=D), wd_hi[:, :, :])
            iteration(0, True, False)
            with dve.Fori(1, B - 1) as i:
                iteration(i, True, True)
            iteration(B - 1, False, True)
            mlp = stepper(mlp_step, (B - 1) * MLP_STEPS)
            mlp_units(B - 1, range(FF_UNITS))
            router(B - 1, *mlp)
            add_shared(B - 1)
            second_norm(B - 1, *mlp)


NEWTON = 3
LN_STEPS = 2 * TT + 3 + 3 * NEWTON

_OUT = ((B, T, D), "float32")


def kernel(**inputs):
    import numpy as np
    import concourse.bacc as bacc
    from concourse.bass_utils import run_bass_kernel_spmd

    a = {n[len("L0_"):]: np.asarray(v) for n, v in inputs.items()}
    gate = np.concatenate([a["ffn_sh_gate"], a["ffn_r_gate"]]).reshape(FF_UNITS, 1, P, D)
    up = np.concatenate([a["ffn_sh_up"], a["ffn_r_up"]]).reshape(FF_UNITS, 1, P, D)
    arrays = {
        "x": a["attn_x"],
        "xT": a["attn_x"].transpose(0, 2, 1),
        "w_proj": np.concatenate([a["attn_Wq1"], a["attn_Wq2"], a["attn_Wk"], a["attn_Wv"], a["attn_Wlam"]], axis=1),
        "w_out": a["attn_Wo"],
        "w_gu": np.concatenate([gate, up], axis=1).reshape(2 * FF_UNITS * P, D).T,
        "w_down": np.concatenate([a["ffn_sh_down"], a["ffn_r_down"]], axis=1).T,
        "w_router": a["ffn_router_weight"].T,
    }
    arrays = {n: np.ascontiguousarray(v) for n, v in arrays.items()}
    nc = bacc.Bacc("TRN2", target_bir_lowering=False, num_devices=1)
    args = {n: nc.dram_tensor(n, v.shape, mybir.dt.from_np(v.dtype), kind="ExternalInput").ap() for n, v in arrays.items()}
    out = nc.dram_tensor("out", _OUT[0], F32, kind="ExternalOutput").ap()
    build_layer(nc, out=out, **args)
    return run_bass_kernel_spmd(nc, [arrays], core_ids=[0]).results[0]["out"]
```

```python
from contextlib import ExitStack

import concourse.bass as bass
from concourse import mybir

P = 128
B, T, D = 8, 256, 256
HEADS = 16
HEAD_DIM = D // HEADS
QHEADS = 2 * HEADS
INTER, MOE_INTER, ROUTED = 1024, 128, 8
TT = T // P
DK = D // P
FF_UNITS = (INTER + MOE_INTER) // P
SHARED_UNITS = INTER // P
QK_BLOCKS = 3 * D // P
Q_BLOCKS = 2 * D // P
QK_JOBS = QK_BLOCKS // 2
BLOCK_HEADS = P // HEAD_DIM
PROJ_COLS = 4 * D + HEADS
Q_PARTS = (0, 0, 0, 1, 1, 2)
K_PARTS = (0, 1, 2, 0, 1, 0)
SLOTS = len(Q_PARTS)
K_RUNS = ((5, 1), (3, 2), (0, 3))
STACK_LOADS = SLOTS + len(K_RUNS)
STACK_ROWS = SLOTS * HEAD_DIM
MAX_PARTS = 2
GROUPS = 8
CONSTS = 5
ROUTER_STEPS = 5
NEWTON = 3
NORM_STATS_STEPS = 2 * TT + 3
LN_STEPS = NORM_STATS_STEPS + (TT + 1) * NEWTON
V_COLS = 32
RING = 3
S_UNITS = QHEADS // 4 + QHEADS // 2
T_UNITS = 3 * GROUPS
DOWN_CHUNKS = 4
QK_AT, SHARED_AT, X1T_AT, ROUTER_AT, ROUTED_AT = (9, 14, 20), (0, 2, 4, 7), 11, 16, 18
FF_LAST_MAX, FF_MAX, FF_SCORES, FF_Y0, FF_Y1, FF_YT = range(0, 1), range(1, 5), range(5, 6), range(6, 7), range(7, 8), range(8, 9)
SPLIT_AT, QK_REST_AT = 5, 2
PROJ_CHUNKS = QK_JOBS + 1
W_PROJ = PROJ_CHUNKS
W_OUT = W_PROJ + 1
W_ROUTER = W_OUT + 1
SCALE = float(HEAD_DIM) ** -0.5
NEG = -3.0e38
EPS = 1e-5
RSQRT_SEED = float(0x5F3759DF - 0x400000)

F32 = mybir.dt.float32
F32R = mybir.dt.float32r
BF16 = mybir.dt.bfloat16
I32 = mybir.dt.int32
ALU = mybir.AluOpType
ACT = mybir.ActivationFunctionType
AX_X = mybir.AxisListType.X


def build_layer(nc, x, xT, w_proj, w_out, w_gu, w_down, w_router, out):
    with ExitStack() as ctx:
        def sb(name, shape, dt=F32):
            return ctx.enter_context(nc.sbuf_tensor(name, shape, dt))

        def sem(name):
            return ctx.enter_context(nc.semaphore(name))

        scratch = nc.dram_tensor("qk_parts_dram", [3, HEAD_DIM, BLOCK_HEADS, QK_BLOCKS, T], BF16, kind="Internal").ap()

        wp_hi, wp_lo = sb("wp_hi", [P, DK, PROJ_COLS], F32R), sb("wp_lo", [P, DK, PROJ_COLS], F32R)
        wo_hi, wo_lo = sb("wo_hi", [P, DK, D], F32R), sb("wo_lo", [P, DK, D], F32R)
        wg_hi, wg_lo = sb("wg_hi", [P, DK, 2 * FF_UNITS * P], F32R), sb("wg_lo", [P, DK, 2 * FF_UNITS * P], F32R)
        wd_hi, wd_lo = sb("wd_hi", [P, FF_UNITS, D], F32R), sb("wd_lo", [P, FF_UNITS, D], F32R)
        wr_hi, wr_lo = sb("wr_hi", [P, DK, P], F32R), sb("wr_lo", [P, DK, P], F32R)
        ident = sb("ident", [P, P])
        ident_b = sb("ident_b", [P, P], BF16)
        mask_b = sb("mask_b", [P, P], BF16)
        xt_raw = sb("xt_raw", [P, DK, T])
        xt_hi, xt_lo = sb("xt_hi", [P, DK, T], F32R), sb("xt_lo", [P, DK, T], F32R)
        parts = sb("parts", [P, 3, QK_BLOCKS, T], BF16)
        rest = sb("rest", [P, QK_JOBS, 2 * T])
        q_stack = sb("q_stack", [P, BLOCK_HEADS, Q_BLOCKS, T], BF16)
        k_stack = sb("k_stack", [P, BLOCK_HEADS, QK_BLOCKS - Q_BLOCKS, T], BF16)
        v_ones = sb("v_ones", [P, TT, HEADS, V_COLS])
        lam_th = sb("lam_th", [P, TT, HEADS])
        lam = sb("lam", [P, TT, HEADS])
        neg_max = sb("neg_max", [P, TT, QHEADS])
        max_parts = sb("max_parts", [QHEADS, MAX_PARTS, T], BF16)
        prob = sb("prob", [P, RING, 3, 2 * T])
        yv = sb("yv", [P, GROUPS, T])
        recip = sb("recip", [P, 3, HEADS])
        y1 = sb("y1", [P, TT, D])
        y2 = sb("y2", [P, TT, D])
        yT_hi, yT_lo = sb("yT_hi", [P, DK, T], F32R), sb("yT_lo", [P, DK, T], F32R)
        x_in = sb("x_in", [P, TT, D])
        z1 = sb("z1", [P, TT, D])
        x1 = sb("x1", [P, TT, D])
        x1T_hi, x1T_lo = sb("x1T_hi", [P, DK, T], F32R), sb("x1T_lo", [P, DK, T], F32R)
        ln_stats = sb("ln_stats", [P, 2, TT, 6])
        ln_mv = sb("ln_mv", [P, 2, TT, 2])
        ln_t = sb("ln_t", [P, 2, 3, TT])
        ln_i = sb("ln_i", [P, 2, TT], I32)
        gate_t = sb("gate_t", [P, RING, T])
        h_full = sb("h_full", [P, RING, T])
        h_hi, h_lo = sb("h_hi", [P, FF_UNITS, T], F32R), sb("h_lo", [P, FF_UNITS, T], F32R)
        logitT = sb("logitT", [ROUTED, T])
        top8 = sb("top8", [P, TT, 8])
        comb = sb("comb", [P, 6, TT])
        z2 = sb("z2", [P, TT, D])
        out_t = sb("out_t", [P, TT, D])

        prob_flat = prob[:, :, :, :].rearrange("p a b c -> p (a b c)")
        wp_raw = prob_flat[:, 0:DK * PROJ_COLS].rearrange("p (k n) -> p k n", k=DK)
        wo_raw, wr_raw = z1[:, :, :], z2[:, :, 0:P]
        gu_cols = 2 * FF_UNITS * P
        yv_cols = GROUPS * T
        GU_PIECES = ((1, slice(0, gu_cols), prob_flat[:, DK * PROJ_COLS:DK * PROJ_COLS + gu_cols]),
                     (0, slice(0, yv_cols), yv[:, :, :].rearrange("p g t -> p (g t)")),
                     (0, slice(yv_cols, gu_cols), out_t[:, 0, 0:gu_cols - yv_cols]))
        wd_raw = sb("wd_raw", [P, FF_UNITS - RING, D])
        DOWN_PIECES = ((slice(0, FF_UNITS - RING), wd_raw[:, :, :]), (slice(FF_UNITS - RING, FF_UNITS), gate_t[:, :, :]))
        W_GATE_UP = len(GU_PIECES)
        W_DOWN = W_GATE_UP + len(DOWN_PIECES)

        def proj_chunk(c):
            return slice(c * 2 * P, (c + 1) * 2 * P if c < QK_JOBS else PROJ_COLS)

        ring = [ctx.enter_context(nc.psum_tensor(f"ring{k}", [P, 512], F32)) for k in range(RING)]
        ybank = [ctx.enter_context(nc.psum_tensor(f"ybank{k}", [P, 512], F32)) for k in range(2)]
        misc = ctx.enter_context(nc.psum_tensor("misc", [P, 512], F32))
        ff = [ctx.enter_context(nc.psum_tensor(f"ff{k}", [P, 512], F32)) for k in range(2)]

        xt_loaded, x_loaded = sem("xt_loaded"), sem("x_loaded")
        wp_loaded = [sem(f"wp{c}_loaded") for c in range(PROJ_CHUNKS)]
        wo_loaded, wr_loaded = sem("wo_loaded"), sem("wr_loaded")
        wg_loaded = [sem(f"wg{n}_loaded") for n in range(len(GU_PIECES))]
        wd_loaded = [sem(f"wd{n}_loaded") for n in range(len(DOWN_PIECES))]
        parts_stored = [sem(f"parts{p}_stored") for p in range(3)]
        stack_loaded, max_loaded, out_stored = sem("stack_loaded"), sem("max_loaded"), sem("out_stored")
        wait_passed = sem("wait_passed")
        consts_made, const_step = sem("consts_made"), sem("const_step")
        w_hi_done, w_lo_done = sem("w_hi_done"), sem("w_lo_done")
        mlp_w_hi_done, mlp_w_lo_done = sem("mlp_w_hi_done"), sem("mlp_w_lo_done")
        xt_hi_done, xt_lo_done = sem("xt_hi_done"), sem("xt_lo_done")
        qk_full, qk_h_done, qk_rest_done, qk_m_done, qk_l_done = (sem(n) for n in ("qk_full", "qk_h_done", "qk_rest_done", "qk_m_done", "qk_l_done"))
        v_full, v_copied, v_done = sem("v_full"), sem("v_copied"), sem("v_done")
        s_full, max_done = sem("s_full"), sem("max_done")
        maxT_full, max_h_done, max_l_done = sem("maxT_full"), sem("max_h_done"), sem("max_l_done")
        t_full, exp_done, causal_done, pv_full, yv_done = (sem(n) for n in ("t_full", "exp_done", "causal_done", "pv_full", "yv_done"))
        y1_full, y2_full, y1_done, y2_done, y_done = (sem(n) for n in ("y1_full", "y2_full", "y1_done", "y2_done", "y_done"))
        yT_full, yT_hi_done, yT_lo_done, wo_full, z1_done = (sem(n) for n in ("yT_full", "yT_hi_done", "yT_lo_done", "wo_full", "z1_done"))
        x1_done, x1T_full, x1T_hi_done, x1T_lo_done, residual_done = (sem(n) for n in ("x1_done", "x1T_full", "x1T_hi_done", "x1T_lo_done", "residual_done"))
        attn_step = sem("attn_step")
        gu_full, gate_th_done, gate_done, h_done, h_hi_done, h_lo_done = (sem(n) for n in ("gu_full", "gate_th_done", "gate_done", "h_done", "h_hi_done", "h_lo_done"))
        logitT_full, logitT_done, logit_full, top_done, top_exp_done = (sem(n) for n in ("logitT_full", "logitT_done", "logit_full", "top_done", "top_exp_done"))
        shared_full, routed_full, z2_shared_done, z2_done, out_done = (sem(n) for n in ("shared_full", "routed_full", "z2_shared_done", "z2_done", "out_done"))
        router_step, norm2_step = sem("router_step"), sem("norm2_step")
        ATTN_STEPS = 1 + 3 * TT + LN_STEPS

        def is_first(b):
            return isinstance(b, int) and b == 0

        def qk_bank(b, n):
            return misc if is_first(b) and n == QK_JOBS - 1 else ybank[(n + 1) % 2]

        def own_wait(eng):
            eng.sem_inc(wait_passed, 1)

        block = ctx.enter_context(nc.Block())

        @block.sync
        def _(sp):
            def load_xt(b):
                if not is_first(b):
                    sp.wait_ge(xt_hi_done, b)
                    sp.wait_ge(xt_lo_done, b)
                    own_wait(sp)
                sp.dma_start(xt_raw[:, :, :], xT[b].rearrange("(k p) t -> p k t", p=P)).then_inc(xt_loaded, 16)

            def store_part(b, n, p):
                sp.wait_ge((qk_h_done, qk_m_done, qk_l_done)[p], b * QK_JOBS + n + 1)
                sp.dma_start(scratch[p].rearrange("d r b t -> r d b t")[:, :, 2 * n:2 * n + 2, :],
                             parts[:, p, 2 * n:2 * n + 2, :]).then_inc(parts_stored[p], 16)

            def store_parts(b, jobs):
                for n in jobs:
                    for p in range(3):
                        store_part(b, n, p)

            def load_stacks(b, p):
                sp.wait_ge(parts_stored[p], (b + 1) * (16 * QK_JOBS))
                own_wait(sp)
                for s in range(SLOTS):
                    if Q_PARTS[s] == p:
                        sp.dma_start(q_stack[HEAD_DIM * s:HEAD_DIM * (s + 1), :, :, :], scratch[p, :, :, 0:Q_BLOCKS, :]).then_inc(stack_loaded, 16)
                s, count = K_RUNS[p]
                sp.dma_start(k_stack[HEAD_DIM * s:HEAD_DIM * (s + count), :, :, :],
                             scratch[0:count, :, :, Q_BLOCKS:QK_BLOCKS, :].rearrange("p d r b t -> (p d) r b t")).then_inc(stack_loaded, 16)

            def load_max(b):
                for p, made in enumerate((max_h_done, max_l_done)):
                    sp.wait_ge(made, b + 1)
                    sp.dma_start(q_stack[STACK_ROWS + p:STACK_ROWS + p + 1, :, :, :], max_parts[:, p, :]).then_inc(max_loaded, 16)

            def load_x(b):
                if not is_first(b):
                    sp.wait_ge(z1_done, b)
                    own_wait(sp)
                sp.dma_start(x_in[:, :, :], x[b].rearrange("(t p) d -> p t d", p=P)).then_inc(x_loaded, 16)

            def store_out(b):
                sp.wait_ge(out_done, (b + 1) * TT)
                own_wait(sp)
                sp.dma_start(out[b].rearrange("(t p) d -> p t d", p=P), out_t[:, :, :]).then_inc(out_stored, 16)

            def iteration(i, has_next=True, has_last=True):
                if has_next and not is_first(i):
                    load_xt(i + 1)
                load_x(i)
                if has_next:
                    store_parts(i + 1, range(QK_JOBS - 1))
                load_max(i)
                if has_next:
                    store_parts(i + 1, range(QK_JOBS - 1, QK_JOBS))
                if is_first(i):
                    for n, (units, raw) in enumerate(DOWN_PIECES):
                        sp.dma_start(raw, w_down.rearrange("(n p) d -> p n d", p=P)[:, units, :]).then_inc(wd_loaded[n], 16)
                if has_last:
                    store_out(i - 2)
                if has_next:
                    sp.wait_ge(t_full, (i + 1) * T_UNITS)
                    for p in range(3):
                        load_stacks(i + 1, p)

            sp.sem_inc(out_stored, 16)
            load_xt(0)
            stage = prob[:, :, :, :].rearrange("p a b c -> p (a b c)")
            for c in range(PROJ_CHUNKS):
                cols = proj_chunk(c)
                sp.dma_start(wp_raw[:, :, cols], w_proj[:, cols].rearrange("(k p) n -> p k n", p=P)).then_inc(wp_loaded[c], 16)
            sp.dma_start(wo_raw, w_out.rearrange("(k p) n -> p k n", p=P)).then_inc(wo_loaded, 16)
            sp.wait_ge(consts_made, 1)
            sp.dma_start(wr_raw[:, :, 0:ROUTED], w_router.rearrange("(k p) n -> p k n", p=P)).then_inc(wr_loaded, 16)
            for n, p in ((0, 0), (1, 0), (0, 1), (2, 0), (1, 1), (2, 1), (0, 2), (1, 2), (2, 2)):
                store_part(0, n, p)
            for p in range(3):
                load_stacks(0, p)
            load_xt(1)
            for n, (k, cols, raw) in enumerate(GU_PIECES):
                sp.dma_start(raw, w_gu[k * P:(k + 1) * P, cols]).then_inc(wg_loaded[n], 16)
            iteration(0, has_last=False)
            iteration(1, has_last=False)
            with sp.Fori(2, B - 1) as i:
                iteration(i)
            iteration(B - 1, has_next=False)
            store_out(B - 2)
            store_out(B - 1)
            sp.wait_ge(out_stored, 16 * (B + 1))

        @block.gpsimd
        def _(pool):
            pool.memset(z2[:, :, :], 0.0).then_inc(consts_made, 1)
            pool.wait_ge(consts_made, 1)
            pool.memset(k_stack[STACK_ROWS:STACK_ROWS + MAX_PARTS, :, :, :], 1.0).then_inc(const_step, 1)
            pool.wait_ge(const_step, 1)
            pool.memset(ident[:, :], 0.0).then_inc(const_step, 1)
            pool.memset(ident_b[:, :], 0.0).then_inc(const_step, 1)
            pool.memset(mask_b[:, :], 0.0).then_inc(const_step, 1)
            pool.memset(v_ones[:, :, :, HEAD_DIM:V_COLS], 0.0).then_inc(const_step, 1)
            pool.wait_ge(const_step, 5)
            for m in (ident, ident_b):
                pool.affine_select(out=m[:, :], in_=m[:, :], compare_op=ALU.not_equal, fill=1.0, base=0,
                                   pattern=[[-1, P]], channel_multiplier=1).then_inc(consts_made, 1)
            pool.affine_select(out=mask_b[:, :], in_=mask_b[:, :], compare_op=ALU.is_ge, fill=NEG, base=0,
                               pattern=[[-1, P]], channel_multiplier=1).then_inc(consts_made, 1)
            pool.memset(v_ones[:, :, :, HEAD_DIM:HEAD_DIM + 1], 1.0).then_inc(consts_made, 1)

            def third_parts(b, jobs=range(QK_JOBS)):
                if not is_first(b):
                    pool.wait_ge(parts_stored[2], b * (16 * QK_JOBS))
                for n in jobs:
                    pool.wait_ge(qk_m_done, b * QK_JOBS + n + 1)
                    view = "p (b t) -> p b t"
                    pool.tensor_tensor(parts[:, 2, 2 * n:2 * n + 2, :], rest[:, n, :].rearrange(view, b=2),
                                       parts[:, 1, 2 * n:2 * n + 2, :], ALU.subtract).then_inc(qk_l_done, 1)

            def split_weight(n, lo, raw, hi):
                pool.wait_ge(mlp_w_hi_done, n)
                pool.tensor_tensor(lo, raw, hi.bitcast(F32), ALU.subtract).then_inc(mlp_w_lo_done, 1)

            def h_rests(b, units):
                for n in units:
                    pool.wait_ge(h_hi_done, b * FF_UNITS + n + 1)
                    pool.tensor_tensor(h_lo[:, n, :], h_full[:, n % RING, :], h_hi[:, n, :].bitcast(F32),
                                       ALU.subtract).then_inc(h_lo_done, 1)

            def causal(b, groups):
                for g in groups:
                    first = prob[:, g % RING, 0:2, :].rearrange("p x (h q) -> p (x h) q", h=2)[:, :, 0:P]
                    last = prob[:, g % RING, 2, :].rearrange("p (h q) -> p h q", q=P)
                    for units, v in ((2, first), (3, last)):
                        pool.wait_ge(exp_done, b * T_UNITS + 3 * g + units)
                        own_wait(pool)
                        pool.affine_select(out=v, in_=v, compare_op=ALU.is_ge, fill=0.0, base=0,
                                           pattern=[[0, 4], [1, P]], channel_multiplier=-1).then_inc(causal_done, 1)

            def iteration(i, has_next, has_prev):
                if is_first(i):
                    for n, (k, cols, raw) in enumerate(GU_PIECES):
                        split_weight(n + 1, wg_lo[:, k, cols], raw, wg_hi[:, k, cols])
                if has_next:
                    third_parts(i + 1, range(QK_JOBS - 1))
                last = FF_MAX[-1]
                if has_prev:
                    h_rests(i - 1, range(last))
                if has_next:
                    third_parts(i + 1, range(QK_JOBS - 1, QK_JOBS))
                causal(i, range(0, 1))
                if has_prev:
                    h_rests(i - 1, range(last, last + 1))
                causal(i, range(1, GROUPS))
                if has_prev:
                    h_rests(i - 1, range(last + 1, FF_UNITS))
                if is_first(i):
                    for n, (units, raw) in enumerate(DOWN_PIECES):
                        split_weight(W_GATE_UP + n + 1, wd_lo[:, units, :], raw, wd_hi[:, units, :])

            third_parts(0)
            iteration(0, True, False)
            iteration(1, True, True)
            with pool.Fori(2, B - 1) as i:
                iteration(i, True, True)
            iteration(B - 1, False, True)
            h_rests(B - 1, range(FF_UNITS))

        @block.scalar
        def _(act):
            def copy(o, i):
                return nc.scalar.activation(o, i, ACT.Copy)

            def split_xt(b):
                act.wait_ge(xt_loaded, (b + 1) * 16)
                copy(xt_hi[:, :, :], xt_raw[:, :, :]).then_inc(xt_hi_done, 1)

            def first_part(b, n):
                act.wait_ge(qk_full, b * QK_JOBS + n + 1)
                copy(parts[:, 0, 2 * n:2 * n + 2, :], qk_bank(b, n)[:, :].rearrange("p (b t) -> p b t", b=2)).then_inc(qk_h_done, 1)

            def second_part(b, n):
                act.wait_ge(qk_rest_done, b * QK_JOBS + n + 1)
                copy(parts[:, 1, 2 * n:2 * n + 2, :], rest[:, n, :].rearrange("p (b t) -> p b t", b=2)).then_inc(qk_m_done, 1)

            def values(b, t):
                act.wait_ge(v_full, b * TT + t + 1)
                copy(v_ones[:, t, :, 0:HEAD_DIM], ring[1 + t][:, 0:D].rearrange("p (h d) -> p h d", h=HEADS)).then_inc(v_copied, 1)
                act.activation(lam_th[:, t, :], ring[1 + t][:, D:D + HEADS], ACT.Tanh, scale=0.5).then_inc(v_done, 1)

            def max_first(b):
                act.wait_ge(maxT_full, b + 1)
                if not is_first(b):
                    act.wait_ge(max_loaded, b * (16 * MAX_PARTS))
                copy(max_parts[:, 0, :], misc[0:QHEADS, 0:T]).then_inc(max_h_done, 1)

            def exps(b, g, units=range(3)):
                for u in units:
                    act.wait_ge(t_full, b * T_UNITS + 3 * g + u + 1)
                    if u == 0 and g >= RING:
                        act.wait_ge(pv_full, b * GROUPS + g - RING + 1)
                    act.activation(prob[:, g % RING, u, :], ring[u][:, :], ACT.Exp, scale=SCALE).then_inc(exp_done, 1)

            def gate_tanh(b, n):
                act.wait_ge(gu_full, b * FF_UNITS + n + 1)
                if is_first(b) and n == 0:
                    act.wait_ge(mlp_w_lo_done, W_DOWN)
                if n >= RING:
                    act.wait_ge(h_done, b * FF_UNITS + n - RING + 1)
                act.activation(gate_t[:, n % RING, :], ff[n % 2][:, 0:T], ACT.Tanh, scale=0.5).then_inc(gate_th_done, 1)

            def h_first(b, n):
                act.wait_ge(h_done, b * FF_UNITS + n + 1)
                copy(h_hi[:, n, :], h_full[:, n % RING, :]).then_inc(h_hi_done, 1)

            def gate_tanhs(b, units):
                for n in units:
                    gate_tanh(b, n)

            def mlp_units(b, units):
                for n in units:
                    gate_tanh(b, n)
                    if n > 0:
                        h_first(b, n - 1)

            def yT_first(b):
                act.wait_ge(yT_full, b + 1)
                copy(yT_hi[:, :, :], misc[:, :].rearrange("p (k t) -> p k t", k=DK)).then_inc(yT_hi_done, 1)

            def residual(b):
                act.wait_ge(x1_done, (b + 1) * TT)
                if not is_first(b):
                    act.wait_ge(out_done, b * TT)
                copy(z2[:, :, :], x1[:, :, :]).then_inc(residual_done, 1)

            def x1T_first(b):
                act.wait_ge(x1T_full, b + 1)
                copy(x1T_hi[:, :, :], misc[:, :].rearrange("p (k t) -> p k t", k=DK)).then_inc(x1T_hi_done, 1)

            def router(b, bank=ff[0]):
                act.wait_ge(logitT_full, b + 1)
                copy(logitT[:, :], bank[0:ROUTED, 0:T]).then_inc(logitT_done, 1)

            def router_exp(b):
                act.wait_ge(router_step, b * ROUTER_STEPS + 1)
                act.activation(comb[:, 1, :], comb[:, 0, :], ACT.Exp).then_inc(top_exp_done, 1)

            def iteration(i, has_next=True, has_prev=True):
                if has_next:
                    split_xt(i + 1)
                    for p in range(2):
                        act.wait_ge(parts_stored[p], (i + 1) * (16 * QK_JOBS))
                for u in range(S_UNITS):
                    if is_first(i) and u == QK_AT[0] + 3:
                        for n, (k, cols, raw) in enumerate(GU_PIECES):
                            split_weight(wg_hi[:, k, cols], raw, wg_loaded[n], mlp_w_hi_done)
                    if has_next:
                        if u in QK_AT:
                            first_part(i + 1, QK_AT.index(u))
                        if u - 2 in QK_AT[:-1]:
                            second_part(i + 1, QK_AT.index(u - 2))
                    if has_prev:
                        if u == X1T_AT:
                            x1T_first(i - 1)
                        if u == ROUTER_AT:
                            router(i - 1)
                max_first(i)
                if has_prev:
                    mlp_units(i - 1, FF_LAST_MAX)
                    router_exp(i - 1)
                    mlp_units(i - 1, FF_MAX)
                if has_next:
                    second_part(i + 1, QK_JOBS - 1)
                if is_first(i):
                    act.wait_ge(mlp_w_lo_done, 1)
                exps(i, 0)
                if has_prev:
                    h_first(i - 1, FF_MAX[-1])
                exps(i, 1)
                if has_prev:
                    gate_tanhs(i - 1, FF_SCORES)
                for g in range(2, GROUPS):
                    exps(i, g)
                if is_first(i):
                    for n, (units, raw) in enumerate(DOWN_PIECES):
                        split_weight(wd_hi[:, units, :], raw, wd_loaded[n], mlp_w_hi_done)
                if has_prev:
                    residual(i - 1)
                    mlp_units(i - 1, FF_Y0)
                    mlp_units(i - 1, FF_Y1)
                if has_next:
                    values(i + 1, 0)
                yT_first(i)
                if has_prev:
                    mlp_units(i - 1, FF_YT)
                if has_next:
                    values(i + 1, 1)
                if has_prev:
                    h_first(i - 1, FF_UNITS - 1)

            def split_weight(hi, raw, loaded, done=w_hi_done):
                act.wait_ge(loaded, 16)
                copy(hi, raw).then_inc(done, 1)

            split_xt(0)
            for c in range(QK_JOBS):
                split_weight(wp_hi[:, :, proj_chunk(c)], wp_raw[:, :, proj_chunk(c)], wp_loaded[c])
                if c > 0:
                    first_part(0, c - 1)
            split_weight(wp_hi[:, :, proj_chunk(QK_JOBS)], wp_raw[:, :, proj_chunk(QK_JOBS)], wp_loaded[QK_JOBS])
            second_part(0, 0)
            first_part(0, QK_JOBS - 1)
            for n in range(1, QK_JOBS):
                second_part(0, n)
            act.wait_ge(consts_made, CONSTS)
            for t in range(TT):
                values(0, t)
            split_weight(wo_hi[:, :, :], wo_raw, wo_loaded)
            split_weight(wr_hi[:, :, :], wr_raw, wr_loaded)
            iteration(0, has_prev=False)
            iteration(1)
            with act.Fori(2, B - 1) as i:
                iteration(i)
            iteration(B - 1, has_next=False)
            x1T_first(B - 1)
            router(B - 1, ybank[1])
            mlp_units(B - 1, range(1))
            router_exp(B - 1)
            mlp_units(B - 1, range(1, FF_UNITS))
            residual(B - 1)
            h_first(B - 1, FF_UNITS - 1)

        @block.tensor
        def _(pe):
            def product(o, lhs_hi, lhs_lo, rhs_hi, rhs_lo, first, last):
                pe.matmul(o, lhs_lo, rhs_hi, start=first, stop=False)
                pe.matmul(o, lhs_hi, rhs_lo, start=False, stop=False)
                return pe.matmul(o, lhs_hi, rhs_hi, start=False, stop=last)

            def qk_job(b, n):
                if n == 0:
                    pe.wait_ge(xt_hi_done, b + 1)
                    pe.wait_ge(xt_lo_done, b + 1)
                if is_first(b):
                    pe.wait_ge(w_hi_done, n + 1)
                    pe.wait_ge(w_lo_done, n + 1)
                elif n == QK_JOBS - 1:
                    pe.wait_ge(qk_rest_done, b * QK_JOBS + 1)
                elif not isinstance(b, int) or b > 1:
                    if n == 0:
                        pe.wait_ge(y2_done, (b - 1) * TT)
                    else:
                        pe.wait_ge(z1_done, b - 1)
                for h in range(2):
                    f = slice((2 * n + h) * P, (2 * n + h + 1) * P)
                    for k in range(DK):
                        mm = product(qk_bank(b, n)[:, h * T:(h + 1) * T], wp_hi[:, k, f], wp_lo[:, k, f],
                                     xt_hi[:, k, :], xt_lo[:, k, :], k == 0, k == DK - 1)
                mm.then_inc(qk_full, 1)

            def v_job(b, t):
                q = slice(t * P, (t + 1) * P)
                w = slice(3 * D, PROJ_COLS)
                for k in range(DK):
                    mm = product(ring[1 + t][:, 0:D + HEADS], xt_hi[:, k, q], xt_lo[:, k, q], wp_hi[:, k, w], wp_lo[:, k, w],
                                 k == 0, k == DK - 1)
                mm.then_inc(v_full, 1)

            def k_head(rows, h, tokens):
                return k_stack[rows, h % BLOCK_HEADS, h // BLOCK_HEADS, tokens]

            def q_head(rows, h, tokens):
                return q_stack[rows, h % BLOCK_HEADS, h // BLOCK_HEADS, tokens]

            def q_pair(rows, n, tokens):
                h = 2 * n
                return q_stack[rows, h % BLOCK_HEADS:h % BLOCK_HEADS + 2, h // BLOCK_HEADS, tokens]

            def s_unit(b, u):
                if u == 0:
                    if not is_first(b):
                        pe.wait_ge(exp_done, b * T_UNITS - RING + 1)
                elif u < RING:
                    pe.wait_ge(v_done, b * TT + u)
                else:
                    pe.wait_ge(max_done, b * S_UNITS + u - RING + 1)
                bank = ring[u % RING]
                if u < QHEADS // 4:
                    t, heads, keys = 0, range(4 * u, 4 * u + 4), P
                else:
                    n = u - QHEADS // 4
                    t, heads, keys = 1, range(2 * n, 2 * n + 2), T
                o = bank[:, :].rearrange("p (h k) -> p h k", k=keys)
                pe.matmul(o[:, :, keys - P:keys], ident_b[:, :], mask_b[:, :].unsqueeze(1).to_broadcast([P, len(heads), P]),
                          start=True, stop=False, skip_group_check=True)
                for j, h in enumerate(heads):
                    mm = pe.matmul(o[:, j, :], q_head(slice(0, STACK_ROWS), h, slice(t * P, (t + 1) * P)), k_head(slice(0, STACK_ROWS), h // 2, slice(0, keys)),
                                   start=False, stop=True, skip_group_check=True)
                mm.then_inc(s_full, 1)

            def max_job(b, has_prev):
                pe.wait_ge(max_done, b * S_UNITS + S_UNITS)
                if has_prev:
                    pe.wait_ge(x1T_lo_done, b)
                for t in range(TT):
                    mm = pe.transpose(misc[0:QHEADS, t * P:(t + 1) * P], neg_max[:, t, :], ident[:, :])
                mm.then_inc(maxT_full, 1)

            def t_group(b, g):
                rows = slice(0, STACK_ROWS + MAX_PARTS)
                for u in range(3):
                    if g == 0:
                        pe.wait_ge(max_done, b * S_UNITS + S_UNITS - RING + u + 1)
                    else:
                        pe.wait_ge(exp_done, b * T_UNITS + 3 * (g - 1) + u + 1)
                    if u < 2:
                        n = 2 * g + u
                        mm = pe.matmul(ring[u][:, :].rearrange("p (h q) -> p h q", h=2), k_head(rows, n, slice(0, P)),
                                       q_pair(rows, n, slice(0, T)), start=True, stop=True)
                    else:
                        for j in range(2):
                            n = 2 * g + j
                            mm = pe.matmul(ring[u][:, j * T:(j + 1) * T].rearrange("p (h q) -> p h q", h=2), k_head(rows, n, slice(P, T)),
                                           q_pair(rows, n, slice(P, T)), start=True, stop=True)
                    mm.then_inc(t_full, 1)

            def pv_group(b, g, has_next):
                bank = ybank[g % 2]
                if g >= 2:
                    pe.wait_ge(yv_done, b * GROUPS + g - 1)
                elif has_next:
                    pe.wait_ge(qk_rest_done, (b + 2) * QK_JOBS - g)
                elif g == 0:
                    pe.wait_ge(z1_done, b)
                else:
                    pe.wait_ge(y2_done, b * TT)
                for t in range(TT):
                    pe.wait_ge(causal_done, b * (2 * GROUPS) + 2 * g + t + 1)
                    for j in range(4):
                        if t == 0:
                            p = prob[:, g % RING, j // 2, (j % 2) * T:(j % 2 + 1) * T]
                        else:
                            p = prob[:, g % RING, 2, j * P:(j + 1) * P]
                        mm = pe.matmul(bank[V_COLS * j:V_COLS * (j + 1), t * P:T], v_ones[:, t, 2 * g + j // 2, :], p,
                                       start=(t == 0), stop=(t == TT - 1))
                mm.then_inc(pv_full, 1)

            def y_jobs(b, t):
                for k, (done, full) in enumerate(((y1_done, y1_full), (y2_done, y2_full))):
                    if t == 0:
                        pe.wait_ge(yv_done, b * GROUPS + (k + 1) * (GROUPS // 2))
                        pe.wait_ge(yv_done, b * GROUPS + GROUPS - 1 + k)
                    else:
                        pe.wait_ge(done, b * TT + t)
                    for j in range(4):
                        mm = pe.transpose(ybank[k][:, j * P:(j + 1) * P], yv[:, 4 * k + j, t * P:(t + 1) * P], ident[:, :])
                    mm.then_inc(full, 1)

            def yT_job(b):
                pe.wait_ge(max_l_done, b + 1)
                for t in range(TT):
                    pe.wait_ge(y_done, b * TT + t + 1)
                    for k in range(DK):
                        mm = pe.transpose(misc[:, k * T + t * P:k * T + (t + 1) * P], y1[:, t, k * P:(k + 1) * P], ident[:, :])
                mm.then_inc(yT_full, 1)

            def wo_job(b):
                pe.wait_ge(yT_hi_done, b + 1)
                pe.wait_ge(yT_lo_done, b + 1)
                pe.wait_ge(y1_done, (b + 1) * TT)
                if is_first(b):
                    pe.wait_ge(w_hi_done, W_OUT)
                    pe.wait_ge(w_lo_done, W_OUT)
                for t in range(TT):
                    q = slice(t * P, (t + 1) * P)
                    for k in range(DK):
                        mm = product(ybank[0][:, t * D:(t + 1) * D], yT_hi[:, k, q], yT_lo[:, k, q], wo_hi[:, k, :], wo_lo[:, k, :],
                                     k == 0, k == DK - 1)
                mm.then_inc(wo_full, 1)

            def x1T_job(b):
                pe.wait_ge(yT_lo_done, b + 1)
                for t in range(TT):
                    pe.wait_ge(x1_done, b * TT + t + 1)
                    for k in range(DK):
                        mm = pe.transpose(misc[:, k * T + t * P:k * T + (t + 1) * P], x1[:, t, k * P:(k + 1) * P], ident[:, :])
                mm.then_inc(x1T_full, 1)

            def gu_units(b, units):
                for n in units:
                    if n == 0:
                        pe.wait_ge(x1T_hi_done, b + 1)
                        pe.wait_ge(x1T_lo_done, b + 1)
                        pe.wait_ge(logitT_done, b + 1)
                        pe.wait_ge(z2_done, (b + 1) * TT)
                    if n == 1:
                        pe.wait_ge(top_done, (b + 1) * TT)
                    if is_first(b) and n == 0:
                        pe.wait_ge(mlp_w_lo_done, W_GATE_UP)
                    if n > 1:
                        pe.wait_ge(h_done, b * FF_UNITS + n - 1)
                    for j in range(2):
                        f = slice((2 * n + j) * P, (2 * n + j + 1) * P)
                        for k in range(DK):
                            mm = product(ff[n % 2][:, j * T:(j + 1) * T], wg_hi[:, k, f], wg_lo[:, k, f], x1T_hi[:, k, :], x1T_lo[:, k, :],
                                         k == 0, k == DK - 1)
                    mm.then_inc(gu_full, 1)

            def router_job(b, bank=ff[0]):
                pe.wait_ge(x1T_hi_done, b + 1)
                pe.wait_ge(x1T_lo_done, b + 1)
                if not is_first(b):
                    pe.wait_ge(h_done, b * FF_UNITS)
                else:
                    pe.wait_ge(w_hi_done, W_ROUTER)
                    pe.wait_ge(w_lo_done, W_ROUTER)
                for k in range(DK):
                    mm = product(bank[:, 0:T], wr_hi[:, k, :], wr_lo[:, k, :], x1T_hi[:, k, :], x1T_lo[:, k, :], k == 0, k == DK - 1)
                mm.then_inc(logitT_full, 1)

            def logit_job(b, bank=ff[1]):
                if not is_first(b):
                    pe.wait_ge(z2_shared_done, b)
                pe.wait_ge(logitT_done, b + 1)
                own_wait(pe)
                for t in range(TT):
                    mm = pe.transpose(bank[:, t * ROUTED:(t + 1) * ROUTED], logitT[:, t * P:(t + 1) * P], ident[0:ROUTED, 0:ROUTED])
                mm.then_inc(logit_full, 1)

            def down(bank, t, units, first, last):
                for n in units:
                    q = slice(t * P, (t + 1) * P)
                    mm = product(bank[:, t * D:(t + 1) * D], h_hi[:, n, q], h_lo[:, n, q], wd_hi[:, n, :], wd_lo[:, n, :],
                                 n == first, n == last)
                return mm

            def shared_chunk(b, c, bank=ff[1]):
                half = SHARED_UNITS * TT // DOWN_CHUNKS
                t, n = divmod(c * half, SHARED_UNITS)
                if bank is ff[1] and c == 0:
                    pe.wait_ge(h_lo_done, (b + 1) * FF_UNITS)
                elif bank is not ff[1]:
                    pe.wait_ge(h_lo_done, b * FF_UNITS + n + half)
                mm = down(bank, t, range(n, n + half), 0, SHARED_UNITS - 1)
                if c == DOWN_CHUNKS - 1:
                    mm.then_inc(shared_full, 1)

            def routed_job(b, bank=ff[0]):
                if bank is ff[0]:
                    pe.wait_ge(logitT_done, b + 2)
                else:
                    pe.wait_ge(h_lo_done, (b + 1) * FF_UNITS)
                for t in range(TT):
                    mm = down(bank, t, range(SHARED_UNITS, FF_UNITS), SHARED_UNITS, FF_UNITS - 1)
                mm.then_inc(routed_full, 1)

            def iteration(i, has_next=True, has_prev=True, has_last=True):
                pe.wait_ge(stack_loaded, (i + 1) * (16 * STACK_LOADS))
                for u in range(S_UNITS):
                    s_unit(i, u)
                    if has_next and u in QK_AT:
                        qk_job(i + 1, QK_AT.index(u))
                    if has_last and u in SHARED_AT:
                        shared_chunk(i - 2, SHARED_AT.index(u))
                    if has_prev and u == X1T_AT:
                        x1T_job(i - 1)
                    if has_prev and u == ROUTER_AT:
                        router_job(i - 1)
                    if has_last and u == ROUTED_AT:
                        routed_job(i - 2)
                if has_prev:
                    gu_units(i - 1, FF_LAST_MAX)
                    logit_job(i - 1)
                max_job(i, has_prev)
                if has_prev:
                    gu_units(i - 1, FF_MAX)
                pe.wait_ge(max_loaded, (i + 1) * (16 * MAX_PARTS))
                for g in range(GROUPS + 2):
                    if g < GROUPS:
                        t_group(i, g)
                    if g == 0 and has_prev:
                        gu_units(i - 1, FF_SCORES)
                    if g >= 2:
                        pv_group(i, g - 2, has_next)
                y_jobs(i, 0)
                if has_prev:
                    gu_units(i - 1, FF_Y0)
                y_jobs(i, 1)
                if has_prev:
                    gu_units(i - 1, FF_Y1)
                if has_next:
                    v_job(i + 1, 0)
                yT_job(i)
                if has_prev:
                    gu_units(i - 1, FF_YT)
                if has_next:
                    v_job(i + 1, 1)
                wo_job(i)

            for n in range(QK_JOBS):
                qk_job(0, n)
            pe.wait_ge(w_hi_done, W_PROJ)
            pe.wait_ge(w_lo_done, W_PROJ)
            for t in range(TT):
                v_job(0, t)
            pe.wait_ge(consts_made, CONSTS)
            iteration(0, has_prev=False, has_last=False)
            iteration(1, has_last=False)
            pe.wait_ge(mlp_w_lo_done, W_DOWN)
            with pe.Fori(2, B - 1) as i:
                iteration(i)
            iteration(B - 1, has_next=False)
            for c in range(DOWN_CHUNKS - 1):
                shared_chunk(B - 2, c)
            routed_job(B - 2, ring[1])
            x1T_job(B - 1)
            shared_chunk(B - 2, DOWN_CHUNKS - 1)
            router_job(B - 1, ybank[1])
            gu_units(B - 1, range(0, 1))
            logit_job(B - 1, ybank[0])
            gu_units(B - 1, range(1, FF_UNITS))
            for c in range(DOWN_CHUNKS):
                shared_chunk(B - 1, c, ring[0])
            routed_job(B - 1, ring[2])

        @block.vector
        def _(dve):
            def stepper(semaphore, done):
                count = [done]

                def step(ins):
                    count[0] = count[0] + 1
                    ins.then_inc(semaphore, 1)

                def settle():
                    dve.wait_ge(semaphore, count[0])
                return step, settle

            def norm_stats(which, z, step, settle):
                stats, mv = ln_stats[:, which], ln_mv[:, which]
                half_var, r, seed = ln_t[:, which, 0, :], ln_t[:, which, 1, :], ln_i[:, which, :]
                for t in range(TT):
                    step(dve.bn_stats(stats[:, t, :], z[:, t, :]))
                settle()
                own_wait(dve)
                for t in range(TT):
                    step(dve.bn_aggr(mv[:, t, :], stats[:, t, :]))
                settle()
                step(dve.tensor_scalar(half_var, mv[:, :, 1], EPS, 0.5, ALU.add, ALU.mult))
                settle()
                step(dve.tensor_scalar(seed, half_var.bitcast(I32), 1, None, ALU.logical_shift_right))
                settle()
                step(dve.tensor_scalar(r.bitcast(I32), seed, -1.0, RSQRT_SEED, ALU.mult, ALU.add))

            def norm_newton(which, step, settle):
                half_var, r, a = ln_t[:, which, 0, :], ln_t[:, which, 1, :], ln_t[:, which, 2, :]
                settle()
                for t in range(TT):
                    step(dve.scalar_tensor_tensor(a[:, t:t + 1], r[:, t:t + 1], r[:, t:t + 1], half_var[:, t:t + 1], ALU.mult, ALU.mult))
                settle()
                step(dve.scalar_tensor_tensor(r, a, 1.5, r, ALU.subtract, ALU.mult, reverse0=True))

            def norm_apply(which, z, y, y_sem, step, settle):
                settle()
                for t in range(TT):
                    dve.tensor_scalar(y[:, t, :], z[:, t, :], ln_mv[:, which, t, 0:1], ln_t[:, which, 1, t:t + 1], ALU.subtract,
                                      ALU.mult).then_inc(y_sem, 1)

            def split_xt(b):
                dve.wait_ge(xt_hi_done, b + 1)
                dve.tensor_tensor(xt_lo[:, :, :], xt_raw[:, :, :], xt_hi[:, :, :].bitcast(F32), ALU.subtract).then_inc(xt_lo_done, 1)

            def qk_rest(b, n):
                dve.wait_ge(qk_h_done, b * QK_JOBS + n + 1)
                dve.tensor_tensor(rest[:, n, :].rearrange("p (b t) -> p b t", b=2), qk_bank(b, n)[:, :].rearrange("p (b t) -> p b t", b=2),
                                  parts[:, 0, 2 * n:2 * n + 2, :], ALU.subtract).then_inc(qk_rest_done, 1)

            def row_max(b, u):
                dve.wait_ge(s_full, b * S_UNITS + u + 1)
                if u < QHEADS // 4:
                    o, keys = neg_max[:, 0, 4 * u:4 * u + 4], P
                else:
                    n = u - QHEADS // 4
                    o, keys = neg_max[:, 1, 2 * n:2 * n + 2], T
                dve.tensor_reduce(o, ring[u % RING][:, :].rearrange("p (h k) -> p h k", k=keys), AX_X, ALU.max,
                                  negate=True).then_inc(max_done, 1)

            def max_second(b):
                dve.wait_ge(max_h_done, b + 1)
                dve.tensor_tensor(max_parts[:, 1, :], misc[0:QHEADS, 0:T], max_parts[:, 0, :], ALU.subtract).then_inc(max_l_done, 1)

            def mlp_unit(b, n):
                dve.wait_ge(gate_th_done, b * FF_UNITS + n + 1)
                dve.scalar_tensor_tensor(gate_t[:, n % RING, :], gate_t[:, n % RING, :], 1.0, ff[n % 2][:, 0:T], ALU.add,
                                         ALU.mult).then_inc(gate_done, 1)
                dve.wait_ge(gate_done, b * FF_UNITS + n + 1)
                if n >= RING:
                    dve.wait_ge(h_lo_done, b * FF_UNITS + n - RING + 1)
                dve.scalar_tensor_tensor(h_full[:, n % RING, :], gate_t[:, n % RING, :], 0.5, ff[n % 2][:, T:2 * T], ALU.mult,
                                         ALU.mult).then_inc(h_done, 1)

            def evacuate_pv(b, g):
                dve.wait_ge(pv_full, b * GROUPS + g + 1)
                dve.tensor_copy(yv[:, g, :], ybank[g % 2][:, 0:T]).then_inc(yv_done, 1)

            def normalize_y(b, t, step, settle):
                def heads(bank):
                    return bank[:, :].rearrange("p (h c) -> p h c", c=V_COLS)

                def wide(r):
                    return r.unsqueeze(2).to_broadcast([P, HEADS, HEAD_DIM])

                dve.wait_ge(y1_full, b * TT + t + 1)
                step(dve.reciprocal(recip[:, 0, :], heads(ybank[0])[:, :, HEAD_DIM]))
                dve.wait_ge(y2_full, b * TT + t + 1)
                step(dve.reciprocal(recip[:, 1, :], heads(ybank[1])[:, :, HEAD_DIM]))
                settle()
                step(dve.tensor_tensor(recip[:, 2, :], recip[:, 1, :], lam[:, t, :], ALU.mult))
                view = "p (h d) -> p h d"
                dve.tensor_tensor(y1[:, t, :].rearrange(view, h=HEADS), heads(ybank[0])[:, :, 0:HEAD_DIM], wide(recip[:, 0, :]),
                                  ALU.mult).then_inc(y1_done, 1)
                settle()
                dve.tensor_tensor(y2[:, t, :].rearrange(view, h=HEADS), heads(ybank[1])[:, :, 0:HEAD_DIM], wide(recip[:, 2, :]),
                                  ALU.mult).then_inc(y2_done, 1)
                dve.wait_ge(y1_done, b * TT + t + 1)
                dve.wait_ge(y2_done, b * TT + t + 1)
                dve.tensor_tensor(y1[:, t, :], y1[:, t, :], y2[:, t, :], ALU.subtract).then_inc(y_done, 1)

            def yT_second(b):
                dve.wait_ge(yT_hi_done, b + 1)
                dve.tensor_tensor(yT_lo[:, :, :], misc[:, :].rearrange("p (k t) -> p k t", k=DK), yT_hi[:, :, :].bitcast(F32),
                                  ALU.subtract).then_inc(yT_lo_done, 1)

            def add_input(b):
                dve.wait_ge(wo_full, b + 1)
                dve.wait_ge(x_loaded, (b + 1) * 16)
                dve.tensor_tensor(z1[:, :, :], ybank[0][:, :].rearrange("p (t d) -> p t d", t=TT), x_in[:, :, :], ALU.add).then_inc(z1_done, 1)
                dve.wait_ge(z1_done, b + 1)

            def x1T_second(b):
                dve.wait_ge(x1T_hi_done, b + 1)
                dve.tensor_tensor(x1T_lo[:, :, :], misc[:, :].rearrange("p (k t) -> p k t", k=DK), x1T_hi[:, :, :].bitcast(F32),
                                  ALU.subtract).then_inc(x1T_lo_done, 1)

            def router_top(b, step, bank=ff[1]):
                dve.wait_ge(logit_full, b + 1)
                own_wait(dve)
                for t in range(TT):
                    dve.max(top8[:, t, :], bank[:, t * ROUTED:(t + 1) * ROUTED]).then_inc(top_done, 1)
                dve.wait_ge(top_done, (b + 1) * TT)
                step(dve.tensor_tensor(comb[:, 0, :], top8[:, :, 1], top8[:, :, 0], ALU.subtract))

            def router_sum(b, step, settle):
                dve.wait_ge(top_exp_done, b + 1)
                step(dve.tensor_scalar(comb[:, 2, :], comb[:, 1, :], 1.0, None, ALU.add))
                settle()
                step(dve.reciprocal(comb[:, 3, :], comb[:, 2, :]))
                settle()
                step(dve.tensor_tensor(comb[:, 4, :], comb[:, 1, :], comb[:, 3, :], ALU.mult))
                settle()
                step(dve.tensor_tensor(comb[:, 5, :], comb[:, 3, :], comb[:, 4, :], ALU.add))

            def add_shared(b, bank=ff[1]):
                dve.wait_ge(shared_full, b + 1)
                dve.wait_ge(residual_done, b + 1)
                dve.tensor_tensor(z2[:, :, :], bank[:, :].rearrange("p (t d) -> p t d", t=TT), z2[:, :, :], ALU.add).then_inc(z2_shared_done, 1)

            def add_routed(b, bank=ff[0]):
                dve.wait_ge(routed_full, b + 1)
                dve.wait_ge(z2_shared_done, b + 1)
                dve.wait_ge(router_step, (b + 1) * ROUTER_STEPS)
                for t in range(TT):
                    dve.scalar_tensor_tensor(z2[:, t, :], bank[:, t * D:(t + 1) * D], comb[:, 5, t:t + 1], z2[:, t, :], ALU.mult,
                                             ALU.add).then_inc(z2_done, 1)
                dve.wait_ge(z2_done, (b + 2) * TT)

            def second_norm_end(b, step, settle):
                if not is_first(b):
                    dve.wait_ge(out_stored, (b + 1) * 16)
                norm_apply(1, z2, out_t, out_done, step, settle)

            def iteration(i, has_next=True, has_prev=True, has_last=True):
                attn = stepper(attn_step, i * ATTN_STEPS)
                router_steps = stepper(router_step, (i - 1) * ROUTER_STEPS)
                norm2 = stepper(norm2_step, (i - 2) * LN_STEPS)
                if has_next:
                    dve.wait_ge(qk_l_done, (i + 1) * QK_JOBS)
                if has_prev:
                    before = stepper(attn_step, i * ATTN_STEPS - LN_STEPS + NORM_STATS_STEPS)
                for u in range(S_UNITS):
                    row_max(i, u)
                    if has_next and u == SPLIT_AT:
                        split_xt(i + 1)
                    if has_prev:
                        if u < NEWTON:
                            norm_newton(0, *before)
                        if u == NEWTON:
                            if has_last:
                                dve.wait_ge(residual_done, i - 1)
                            norm_apply(0, z1, x1, x1_done, *before)
                        if u - 2 == X1T_AT:
                            x1T_second(i - 1)
                    if has_last:
                        if u - 1 == SHARED_AT[-1]:
                            add_shared(i - 2)
                        if u - 1 == ROUTED_AT:
                            add_routed(i - 2)
                    if has_next and u - 1 in QK_AT[:-1]:
                        qk_rest(i + 1, QK_AT.index(u - 1))
                if has_prev:
                    router_top(i - 1, router_steps[0])
                max_second(i)
                attn[0](dve.tensor_scalar(lam[:, :, :], lam_th[:, :, :], 0.5, 0.5, ALU.mult, ALU.add))
                if has_prev:
                    for n in FF_LAST_MAX:
                        mlp_unit(i - 1, n)
                    router_sum(i - 1, *router_steps)
                    for n in FF_MAX:
                        mlp_unit(i - 1, n)
                        if has_next and n == QK_REST_AT:
                            qk_rest(i + 1, QK_JOBS - 1)
                    for n in FF_SCORES:
                        mlp_unit(i - 1, n)
                elif has_next:
                    qk_rest(i + 1, QK_JOBS - 1)
                for g in range(GROUPS):
                    if g == 0 and is_first(i):
                        dve.wait_ge(mlp_w_lo_done, W_GATE_UP)
                    evacuate_pv(i, g)
                    if has_last:
                        if g == 0:
                            norm_stats(1, z2, *norm2)
                        elif g <= NEWTON:
                            norm_newton(1, *norm2)
                        elif g == NEWTON + 1:
                            second_norm_end(i - 2, *norm2)
                normalize_y(i, 0, *attn)
                if has_prev:
                    for n in FF_Y0:
                        mlp_unit(i - 1, n)
                normalize_y(i, 1, *attn)
                if has_prev:
                    for n in FF_Y1:
                        mlp_unit(i - 1, n)
                yT_second(i)
                if has_prev:
                    for n in FF_YT:
                        mlp_unit(i - 1, n)
                add_input(i)
                norm_stats(0, z1, *attn)

            def split_weight(n, lo, raw, hi):
                dve.wait_ge(w_hi_done, n)
                dve.tensor_tensor(lo, raw, hi.bitcast(F32), ALU.subtract).then_inc(w_lo_done, 1)

            dve.sem_inc(z2_done, TT)
            split_xt(0)
            for c in range(QK_JOBS):
                split_weight(c + 1, wp_lo[:, :, proj_chunk(c)], wp_raw[:, :, proj_chunk(c)], wp_hi[:, :, proj_chunk(c)])
                if c > 0:
                    qk_rest(0, c - 1)
            split_weight(W_PROJ, wp_lo[:, :, proj_chunk(QK_JOBS)], wp_raw[:, :, proj_chunk(QK_JOBS)], wp_hi[:, :, proj_chunk(QK_JOBS)])
            qk_rest(0, QK_JOBS - 1)
            split_weight(W_OUT, wo_lo[:, :, :], wo_raw, wo_hi[:, :, :])
            split_weight(W_ROUTER, wr_lo[:, :, :], wr_raw, wr_hi[:, :, :])
            iteration(0, has_prev=False, has_last=False)
            iteration(1, has_last=False)
            with dve.Fori(2, B - 1) as i:
                iteration(i)
            iteration(B - 1, has_next=False)

            first = stepper(attn_step, B * ATTN_STEPS - LN_STEPS + NORM_STATS_STEPS)
            for _ in range(NEWTON):
                norm_newton(0, *first)
            dve.wait_ge(residual_done, B - 1)
            norm_apply(0, z1, x1, x1_done, *first)
            x1T_second(B - 1)
            add_shared(B - 2)
            add_routed(B - 2, ring[1])
            last_router = stepper(router_step, (B - 1) * ROUTER_STEPS)
            router_top(B - 1, last_router[0], ybank[0])
            norm2 = stepper(norm2_step, (B - 2) * LN_STEPS)
            for n in range(FF_UNITS):
                mlp_unit(B - 1, n)
                if n == 0:
                    router_sum(B - 1, *last_router)
                if n == 1:
                    norm_stats(1, z2, *norm2)
                if 1 < n < NEWTON + 2:
                    norm_newton(1, *norm2)
                if n == NEWTON + 2:
                    second_norm_end(B - 2, *norm2)
            add_shared(B - 1, ring[0])
            add_routed(B - 1, ring[2])
            norm2 = stepper(norm2_step, (B - 1) * LN_STEPS)
            norm_stats(1, z2, *norm2)
            for _ in range(NEWTON):
                norm_newton(1, *norm2)
            second_norm_end(B - 1, *norm2)


_OUT = ((B, T, D), "float32")


def kernel(**inputs):
    import numpy as np
    import concourse.bacc as bacc
    from concourse.bass_utils import run_bass_kernel_spmd

    a = {n[len("L0_"):]: np.asarray(v) for n, v in inputs.items()}
    gate = np.concatenate([a["ffn_sh_gate"], a["ffn_r_gate"]]).reshape(FF_UNITS, 1, P, D)
    up = np.concatenate([a["ffn_sh_up"], a["ffn_r_up"]]).reshape(FF_UNITS, 1, P, D)
    arrays = {
        "x": a["attn_x"],
        "xT": a["attn_x"].transpose(0, 2, 1),
        "w_proj": np.concatenate([a["attn_Wq1"], a["attn_Wq2"], a["attn_Wk"], a["attn_Wv"], a["attn_Wlam"]], axis=1),
        "w_out": a["attn_Wo"],
        "w_gu": np.concatenate([gate, up], axis=1).reshape(2 * FF_UNITS * P, D).T,
        "w_down": np.concatenate([a["ffn_sh_down"], a["ffn_r_down"]], axis=1).T,
        "w_router": a["ffn_router_weight"].T,
    }
    arrays = {n: np.ascontiguousarray(v) for n, v in arrays.items()}
    nc = bacc.Bacc("TRN2", target_bir_lowering=False, num_devices=1)
    args = {n: nc.dram_tensor(n, v.shape, mybir.dt.from_np(v.dtype), kind="ExternalInput").ap() for n, v in arrays.items()}
    out = nc.dram_tensor("out", _OUT[0], F32, kind="ExternalOutput").ap()
    build_layer(nc, out=out, **args)
    return run_bass_kernel_spmd(nc, [arrays], core_ids=[0]).results[0]["out"]
```

```python
from contextlib import ExitStack

import concourse.bass as bass
from concourse import mybir

P = 128
B, T, D = 8, 256, 256
HEADS = 16
HEAD_DIM = D // HEADS
QHEADS = 2 * HEADS
INTER, MOE_INTER, ROUTED = 1024, 128, 8
TT = T // P
DK = D // P
FF_UNITS = (INTER + MOE_INTER) // P
SHARED_UNITS = INTER // P
QK_BLOCKS = 3 * D // P
Q_BLOCKS = 2 * D // P
QK_JOBS = QK_BLOCKS // 2
BLOCK_HEADS = P // HEAD_DIM
PROJ_COLS = 4 * D + HEADS
Q_PARTS = (0, 0, 0, 1, 1, 2)
K_PARTS = (0, 1, 2, 0, 1, 0)
SLOTS = len(Q_PARTS)
K_RUNS = ((5, 1), (3, 2), (0, 3))
STACK_LOADS = SLOTS + len(K_RUNS)
STACK_ROWS = SLOTS * HEAD_DIM
MAX_PARTS = 2
GROUPS = 8
CONSTS = 5
ROUTER_STEPS = 5
NEWTON = 3
LN_STEPS = 2 * TT + 3 + (TT + 1) * NEWTON
NORM1_STEPS = LN_STEPS + 1
V_COLS = 32
RING = 3
S_UNITS = QHEADS // 4 + QHEADS // 2
T_UNITS = 3 * GROUPS
DOWN_CHUNKS = 4
QK_AT = 4
APPLY_AT, X1T_AT, ROUTER_AT, LOGIT_AT = 7, 11, 16, 20
SHARED_AT, ROUTED_AT = (1, 5, 8, 13), 19
FF_FIRST, FF_MAX, FF_SCORES, FF_Y0, FF_Y1, FF_YT = 0, range(1, 5), 5, 6, 7, 8
FF_SCORES_GROUP = 1
QK_GROUPS = (0, 2)
PROJ_CHUNKS = QK_JOBS + 1
W_PROJ = PROJ_CHUNKS
W_OUT = W_PROJ + 1
W_ROUTER = W_OUT + 1
SCALE = float(HEAD_DIM) ** -0.5
NEG = -3.0e38
EPS = 1e-5
RSQRT_SEED = float(0x5F3759DF - 0x400000)

F32 = mybir.dt.float32
F32R = mybir.dt.float32r
BF16 = mybir.dt.bfloat16
I32 = mybir.dt.int32
ALU = mybir.AluOpType
ACT = mybir.ActivationFunctionType
AX_X = mybir.AxisListType.X


def build_layer(nc, x, xT, w_proj, w_out, w_gu, w_down, w_router, out):
    with ExitStack() as ctx:
        def sb(name, shape, dt=F32):
            return ctx.enter_context(nc.sbuf_tensor(name, shape, dt))

        def sem(name):
            return ctx.enter_context(nc.semaphore(name))

        scratch = nc.dram_tensor("qk_parts_dram", [3, HEAD_DIM, BLOCK_HEADS, QK_BLOCKS, T], BF16, kind="Internal").ap()

        wp_hi, wp_lo = sb("wp_hi", [P, DK, PROJ_COLS], F32R), sb("wp_lo", [P, DK, PROJ_COLS], F32R)
        wo_hi, wo_lo = sb("wo_hi", [P, DK, D], F32R), sb("wo_lo", [P, DK, D], F32R)
        wg_hi, wg_lo = sb("wg_hi", [P, DK, 2 * FF_UNITS * P], F32R), sb("wg_lo", [P, DK, 2 * FF_UNITS * P], F32R)
        wd_hi, wd_lo = sb("wd_hi", [P, FF_UNITS, D], F32R), sb("wd_lo", [P, FF_UNITS, D], F32R)
        wr_hi, wr_lo = sb("wr_hi", [P, DK, P], F32R), sb("wr_lo", [P, DK, P], F32R)
        ident = sb("ident", [P, P])
        ident_b = sb("ident_b", [P, P], BF16)
        mask_b = sb("mask_b", [P, P], BF16)
        xt_raw = sb("xt_raw", [P, DK, T])
        xt_hi, xt_lo = sb("xt_hi", [P, DK, T], F32R), sb("xt_lo", [P, DK, T], F32R)
        parts = sb("parts", [P, 3, QK_BLOCKS, T], BF16)
        rest = sb("rest", [P, QK_JOBS, 2 * T])
        q_stack = sb("q_stack", [P, BLOCK_HEADS, Q_BLOCKS, T], BF16)
        k_stack = sb("k_stack", [P, BLOCK_HEADS, QK_BLOCKS - Q_BLOCKS, T], BF16)
        v_ones = sb("v_ones", [P, TT, HEADS, V_COLS])
        lam_th = sb("lam_th", [P, TT, HEADS])
        lam = sb("lam", [P, TT, HEADS])
        neg_max = sb("neg_max", [P, TT, QHEADS])
        max_parts = sb("max_parts", [QHEADS, MAX_PARTS, T], BF16)
        prob = sb("prob", [P, RING, 3, 2 * T])
        yv = sb("yv", [P, GROUPS, T])
        recip = sb("recip", [P, 3, HEADS])
        y1 = sb("y1", [P, TT, D])
        y2 = sb("y2", [P, TT, D])
        yT_hi, yT_lo = sb("yT_hi", [P, DK, T], F32R), sb("yT_lo", [P, DK, T], F32R)
        x_in = sb("x_in", [P, TT, D])
        z1 = sb("z1", [P, TT, D])
        x1 = sb("x1", [P, TT, D])
        x1T_hi, x1T_lo = sb("x1T_hi", [P, DK, T], F32R), sb("x1T_lo", [P, DK, T], F32R)
        ln_stats = sb("ln_stats", [P, 2, TT, 6])
        ln_mv = sb("ln_mv", [P, 2, TT, 2])
        ln_t = sb("ln_t", [P, 2, 3, TT])
        ln_shift = sb("ln_shift", [P, TT])
        ln_i = sb("ln_i", [P, 2, TT], I32)
        gate_t = sb("gate_t", [P, RING, T])
        h_full = sb("h_full", [P, RING, T])
        h_hi, h_lo = sb("h_hi", [P, FF_UNITS, T], F32R), sb("h_lo", [P, FF_UNITS, T], F32R)
        logitT = sb("logitT", [ROUTED, T])
        top8 = sb("top8", [P, TT, 8])
        comb = sb("comb", [P, 6, TT])
        z2 = sb("z2", [P, TT, D])
        out_t = sb("out_t", [P, TT, D])

        prob_flat = prob[:, :, :, :].rearrange("p a b c -> p (a b c)")
        wp_raw = prob_flat[:, 0:DK * PROJ_COLS].rearrange("p (k n) -> p k n", k=DK)
        wo_raw, wr_raw = z1[:, :, :], z2[:, :, 0:P]
        gu_cols = 2 * FF_UNITS * P
        yv_cols = GROUPS * T
        GU_PIECES = ((1, slice(0, gu_cols), prob_flat[:, DK * PROJ_COLS:DK * PROJ_COLS + gu_cols]),
                     (0, slice(0, yv_cols), yv[:, :, :].rearrange("p g t -> p (g t)")),
                     (0, slice(yv_cols, gu_cols), out_t[:, 0, 0:gu_cols - yv_cols]))
        wd_raw = sb("wd_raw", [P, FF_UNITS - RING, D])
        shared_out, routed_out = wd_raw[:, 0:TT, :], wd_raw[:, TT:2 * TT, :]
        DOWN_PIECES = ((slice(0, FF_UNITS - RING), wd_raw[:, :, :]), (slice(FF_UNITS - RING, FF_UNITS), gate_t[:, :, :]))
        W_GATE_UP = len(GU_PIECES)
        W_DOWN = W_GATE_UP + len(DOWN_PIECES)

        def proj_chunk(c):
            return slice(c * 2 * P, (c + 1) * 2 * P if c < QK_JOBS else PROJ_COLS)

        ring = [ctx.enter_context(nc.psum_tensor(f"ring{k}", [P, 512], F32)) for k in range(RING)]
        ybank = [ctx.enter_context(nc.psum_tensor(f"ybank{k}", [P, 512], F32)) for k in range(2)]
        misc = ctx.enter_context(nc.psum_tensor("misc", [P, 512], F32))
        ff = [ctx.enter_context(nc.psum_tensor(f"ff{k}", [P, 512], F32)) for k in range(2)]

        xt_loaded, x_loaded = sem("xt_loaded"), sem("x_loaded")
        wp_loaded = [sem(f"wp{c}_loaded") for c in range(PROJ_CHUNKS)]
        wo_loaded, wr_loaded = sem("wo_loaded"), sem("wr_loaded")
        wg_loaded = [sem(f"wg{n}_loaded") for n in range(len(GU_PIECES))]
        wd_loaded = [sem(f"wd{n}_loaded") for n in range(len(DOWN_PIECES))]
        parts_stored = [sem(f"parts{p}_stored") for p in range(3)]
        stack_loaded, max_loaded, out_stored = sem("stack_loaded"), sem("max_loaded"), sem("out_stored")
        wait_passed = sem("wait_passed")
        consts_made, const_step = sem("consts_made"), sem("const_step")
        w_hi_done, w_lo_done = sem("w_hi_done"), sem("w_lo_done")
        mlp_w_hi_done, mlp_w_lo_done = sem("mlp_w_hi_done"), sem("mlp_w_lo_done")
        xt_hi_done, xt_lo_done = sem("xt_hi_done"), sem("xt_lo_done")
        qk_full, qk_h_done, qk_rest_done, qk_m_done, qk_l_done = (sem(n) for n in ("qk_full", "qk_h_done", "qk_rest_done", "qk_m_done", "qk_l_done"))
        v_full, v_copied, v_done = sem("v_full"), sem("v_copied"), sem("v_done")
        s_full, max_done = sem("s_full"), sem("max_done")
        maxT_full, max_h_done, max_l_done = sem("maxT_full"), sem("max_h_done"), sem("max_l_done")
        t_full, exp_done, causal_done, pv_full, yv_done = (sem(n) for n in ("t_full", "exp_done", "causal_done", "pv_full", "yv_done"))
        y1_full, y2_full, y1_done, y2_done, y_done = (sem(n) for n in ("y1_full", "y2_full", "y1_done", "y2_done", "y_done"))
        yT_full, yT_hi_done, yT_lo_done, wo_full, z1_done = (sem(n) for n in ("yT_full", "yT_hi_done", "yT_lo_done", "wo_full", "z1_done"))
        x1_done, x1T_full, x1T_hi_done, x1T_lo_done, residual_done = (sem(n) for n in ("x1_done", "x1T_full", "x1T_hi_done", "x1T_lo_done", "residual_done"))
        attn_step = sem("attn_step")
        gu_full, gate_th_done, gate_done, h_done, h_hi_done, h_lo_done = (sem(n) for n in ("gu_full", "gate_th_done", "gate_done", "h_done", "h_hi_done", "h_lo_done"))
        logitT_full, logitT_done, logit_full, top_done, top_exp_done = (sem(n) for n in ("logitT_full", "logitT_done", "logit_full", "top_done", "top_exp_done"))
        shared_full, routed_full, z2_shared_done, z2_done, out_done = (sem(n) for n in ("shared_full", "routed_full", "z2_shared_done", "z2_done", "out_done"))
        shared_copied, routed_copied = sem("shared_copied"), sem("routed_copied")
        router_step, norm2_step = sem("router_step"), sem("norm2_step")
        ATTN_STEPS = 1 + 3 * TT + NORM1_STEPS

        def is_first(b):
            return isinstance(b, int) and b == 0

        def qk_bank(n):
            return (ybank[0], ybank[1], misc)[n]

        def own_wait(eng):
            eng.sem_inc(wait_passed, 1)

        block = ctx.enter_context(nc.Block())

        @block.sync
        def _(sp):
            def load_xt(b):
                if not is_first(b):
                    sp.wait_ge(xt_hi_done, b)
                    sp.wait_ge(xt_lo_done, b)
                    own_wait(sp)
                sp.dma_start(xt_raw[:, :, :], xT[b].rearrange("(k p) t -> p k t", p=P)).then_inc(xt_loaded, 16)

            def store_part(b, n, p):
                sp.wait_ge((qk_h_done, qk_m_done, qk_l_done)[p], b * QK_JOBS + n + 1)
                sp.dma_start(scratch[p].rearrange("d r b t -> r d b t")[:, :, 2 * n:2 * n + 2, :],
                             parts[:, p, 2 * n:2 * n + 2, :]).then_inc(parts_stored[p], 16)

            def store_parts(b, jobs):
                for n in jobs:
                    for p in range(3):
                        store_part(b, n, p)

            def load_stacks(b, p):
                sp.wait_ge(parts_stored[p], (b + 1) * (16 * QK_JOBS))
                own_wait(sp)
                for s in range(SLOTS):
                    if Q_PARTS[s] == p:
                        sp.dma_start(q_stack[HEAD_DIM * s:HEAD_DIM * (s + 1), :, :, :], scratch[p, :, :, 0:Q_BLOCKS, :]).then_inc(stack_loaded, 16)
                s, count = K_RUNS[p]
                sp.dma_start(k_stack[HEAD_DIM * s:HEAD_DIM * (s + count), :, :, :],
                             scratch[0:count, :, :, Q_BLOCKS:QK_BLOCKS, :].rearrange("p d r b t -> (p d) r b t")).then_inc(stack_loaded, 16)

            def load_max(b):
                for p, made in enumerate((max_h_done, max_l_done)):
                    sp.wait_ge(made, b + 1)
                    sp.dma_start(q_stack[STACK_ROWS + p:STACK_ROWS + p + 1, :, :, :], max_parts[:, p, :]).then_inc(max_loaded, 16)

            def load_x(b):
                if not is_first(b):
                    sp.wait_ge(z1_done, b)
                    own_wait(sp)
                sp.dma_start(x_in[:, :, :], x[b].rearrange("(t p) d -> p t d", p=P)).then_inc(x_loaded, 16)

            def store_out(b):
                sp.wait_ge(out_done, (b + 1) * TT)
                own_wait(sp)
                sp.dma_start(out[b].rearrange("(t p) d -> p t d", p=P), out_t[:, :, :]).then_inc(out_stored, 16)

            def iteration(i, has_next=True, has_last=True):
                if has_next and not is_first(i):
                    load_xt(i + 1)
                load_x(i)
                load_max(i)
                if has_next:
                    store_parts(i + 1, range(QK_JOBS))
                if is_first(i):
                    for n, (units, raw) in enumerate(DOWN_PIECES):
                        sp.dma_start(raw, w_down.rearrange("(n p) d -> p n d", p=P)[:, units, :]).then_inc(wd_loaded[n], 16)
                if has_last:
                    store_out(i - 2)
                if has_next:
                    sp.wait_ge(t_full, (i + 1) * T_UNITS)
                    for p in range(3):
                        load_stacks(i + 1, p)

            sp.sem_inc(out_stored, 16)
            load_xt(0)
            for c in range(PROJ_CHUNKS):
                cols = proj_chunk(c)
                sp.dma_start(wp_raw[:, :, cols], w_proj[:, cols].rearrange("(k p) n -> p k n", p=P)).then_inc(wp_loaded[c], 16)
            sp.dma_start(wo_raw, w_out.rearrange("(k p) n -> p k n", p=P)).then_inc(wo_loaded, 16)
            sp.wait_ge(consts_made, 1)
            sp.dma_start(wr_raw[:, :, 0:ROUTED], w_router.rearrange("(k p) n -> p k n", p=P)).then_inc(wr_loaded, 16)
            for n, p in ((0, 0), (1, 0), (0, 1), (2, 0), (1, 1), (2, 1), (0, 2), (1, 2), (2, 2)):
                store_part(0, n, p)
            for p in range(3):
                load_stacks(0, p)
            load_xt(1)
            for n, (k, cols, raw) in enumerate(GU_PIECES):
                sp.dma_start(raw, w_gu[k * P:(k + 1) * P, cols]).then_inc(wg_loaded[n], 16)
            iteration(0, has_last=False)
            iteration(1, has_last=False)
            with sp.Fori(2, B - 1) as i:
                iteration(i)
            iteration(B - 1, has_next=False)
            store_out(B - 2)
            store_out(B - 1)
            sp.wait_ge(out_stored, 16 * (B + 1))

        @block.gpsimd
        def _(pool):
            pool.memset(z2[:, :, :], 0.0).then_inc(consts_made, 1)
            pool.wait_ge(consts_made, 1)
            pool.memset(k_stack[STACK_ROWS:STACK_ROWS + MAX_PARTS, :, :, :], 1.0).then_inc(const_step, 1)
            pool.wait_ge(const_step, 1)
            pool.memset(ident[:, :], 0.0).then_inc(const_step, 1)
            pool.memset(ident_b[:, :], 0.0).then_inc(const_step, 1)
            pool.memset(mask_b[:, :], 0.0).then_inc(const_step, 1)
            pool.memset(v_ones[:, :, :, HEAD_DIM:V_COLS], 0.0).then_inc(const_step, 1)
            pool.wait_ge(const_step, 5)
            for m in (ident, ident_b):
                pool.affine_select(out=m[:, :], in_=m[:, :], compare_op=ALU.not_equal, fill=1.0, base=0,
                                   pattern=[[-1, P]], channel_multiplier=1).then_inc(consts_made, 1)
            pool.affine_select(out=mask_b[:, :], in_=mask_b[:, :], compare_op=ALU.is_ge, fill=NEG, base=0,
                               pattern=[[-1, P]], channel_multiplier=1).then_inc(consts_made, 1)
            pool.memset(v_ones[:, :, :, HEAD_DIM:HEAD_DIM + 1], 1.0).then_inc(consts_made, 1)

            def split_xt(b):
                pool.wait_ge(xt_hi_done, b + 1)
                pool.tensor_tensor(xt_lo[:, :, :], xt_raw[:, :, :], xt_hi[:, :, :].bitcast(F32), ALU.subtract).then_inc(xt_lo_done, 1)

            def third_parts(b, jobs=range(QK_JOBS)):
                if not is_first(b):
                    pool.wait_ge(parts_stored[2], b * (16 * QK_JOBS))
                for n in jobs:
                    pool.wait_ge(qk_m_done, b * QK_JOBS + n + 1)
                    view = "p (b t) -> p b t"
                    pool.tensor_tensor(parts[:, 2, 2 * n:2 * n + 2, :], rest[:, n, :].rearrange(view, b=2),
                                       parts[:, 1, 2 * n:2 * n + 2, :], ALU.subtract).then_inc(qk_l_done, 1)

            def split_weight(n, lo, raw, hi):
                pool.wait_ge(mlp_w_hi_done, n)
                pool.tensor_tensor(lo, raw, hi.bitcast(F32), ALU.subtract).then_inc(mlp_w_lo_done, 1)

            def h_rests(b, units):
                for n in units:
                    pool.wait_ge(h_hi_done, b * FF_UNITS + n + 1)
                    pool.tensor_tensor(h_lo[:, n, :], h_full[:, n % RING, :], h_hi[:, n, :].bitcast(F32),
                                       ALU.subtract).then_inc(h_lo_done, 1)

            def causal(b, groups):
                for g in groups:
                    first = prob[:, g % RING, 0:2, :].rearrange("p x (h q) -> p (x h) q", h=2)[:, :, 0:P]
                    last = prob[:, g % RING, 2, :].rearrange("p (h q) -> p h q", q=P)
                    for units, v in ((2, first), (3, last)):
                        pool.wait_ge(exp_done, b * T_UNITS + 3 * g + units)
                        own_wait(pool)
                        pool.affine_select(out=v, in_=v, compare_op=ALU.is_ge, fill=0.0, base=0,
                                           pattern=[[0, 4], [1, P]], channel_multiplier=-1).then_inc(causal_done, 1)

            def add_shared(b):
                pool.wait_ge(shared_copied, b + 1)
                pool.wait_ge(residual_done, b + 1)
                pool.tensor_tensor(z2[:, :, :], z2[:, :, :], shared_out, ALU.add).then_inc(z2_shared_done, 1)

            def add_routed(b):
                pool.wait_ge(routed_copied, (b + 1) * TT)
                pool.wait_ge(z2_shared_done, b + 1)
                pool.tensor_tensor(z2[:, :, :], z2[:, :, :], routed_out, ALU.add).then_inc(z2_done, TT)

            def iteration(i, has_next, has_prev, has_last):
                if has_next:
                    split_xt(i + 1)
                if is_first(i):
                    for n, (k, cols, raw) in enumerate(GU_PIECES):
                        split_weight(n + 1, wg_lo[:, k, cols], raw, wg_hi[:, k, cols])
                if has_next:
                    third_parts(i + 1, range(1))
                if has_last:
                    add_shared(i - 2)
                if has_last:
                    add_routed(i - 2)
                last = FF_MAX[-1]
                if has_prev:
                    h_rests(i - 1, range(last))
                causal(i, range(0, 1))
                if has_prev:
                    h_rests(i - 1, range(last, last + 1))
                for g in range(1, GROUPS):
                    causal(i, range(g, g + 1))
                    if has_next and g - 2 in QK_GROUPS:
                        n = 1 + QK_GROUPS.index(g - 2)
                        third_parts(i + 1, range(n, n + 1))
                if has_prev:
                    h_rests(i - 1, range(last + 1, FF_UNITS))
                if is_first(i):
                    for n, (units, raw) in enumerate(DOWN_PIECES):
                        split_weight(W_GATE_UP + n + 1, wd_lo[:, units, :], raw, wd_hi[:, units, :])

            third_parts(0)
            iteration(0, True, False, False)
            iteration(1, True, True, False)
            with pool.Fori(2, B - 1) as i:
                iteration(i, True, True, True)
            iteration(B - 1, False, True, True)
            h_rests(B - 1, range(FF_UNITS))

        @block.scalar
        def _(act):
            def copy(o, i):
                return nc.scalar.activation(o, i, ACT.Copy)

            def split_xt(b):
                act.wait_ge(xt_loaded, (b + 1) * 16)
                copy(xt_hi[:, :, :], xt_raw[:, :, :]).then_inc(xt_hi_done, 1)

            def first_part(b, n):
                act.wait_ge(qk_full, b * QK_JOBS + n + 1)
                copy(parts[:, 0, 2 * n:2 * n + 2, :], qk_bank(n)[:, :].rearrange("p (b t) -> p b t", b=2)).then_inc(qk_h_done, 1)

            def second_part(b, n):
                act.wait_ge(qk_rest_done, b * QK_JOBS + n + 1)
                copy(parts[:, 1, 2 * n:2 * n + 2, :], rest[:, n, :].rearrange("p (b t) -> p b t", b=2)).then_inc(qk_m_done, 1)

            def values(b, t):
                act.wait_ge(v_full, b * TT + t + 1)
                copy(v_ones[:, t, :, 0:HEAD_DIM], ring[1 + t][:, 0:D].rearrange("p (h d) -> p h d", h=HEADS)).then_inc(v_copied, 1)
                act.activation(lam_th[:, t, :], ring[1 + t][:, D:D + HEADS], ACT.Tanh, scale=0.5).then_inc(v_done, 1)

            def max_first(b):
                act.wait_ge(maxT_full, b + 1)
                if not is_first(b):
                    act.wait_ge(max_loaded, b * (16 * MAX_PARTS))
                copy(max_parts[:, 0, :], misc[0:QHEADS, 0:T]).then_inc(max_h_done, 1)

            def exps(b, g, units=range(3)):
                for u in units:
                    act.wait_ge(t_full, b * T_UNITS + 3 * g + u + 1)
                    if u == 0 and g >= RING:
                        act.wait_ge(pv_full, b * GROUPS + g - RING + 1)
                    act.activation(prob[:, g % RING, u, :], ring[u][:, :], ACT.Exp, scale=SCALE).then_inc(exp_done, 1)

            def gate_tanh(b, n):
                act.wait_ge(gu_full, b * FF_UNITS + n + 1)
                if is_first(b) and n == 0:
                    act.wait_ge(mlp_w_lo_done, W_DOWN)
                if n >= RING:
                    act.wait_ge(h_done, b * FF_UNITS + n - RING + 1)
                act.activation(gate_t[:, n % RING, :], ff[n % 2][:, 0:T], ACT.Tanh, scale=0.5).then_inc(gate_th_done, 1)

            def h_first(b, n):
                act.wait_ge(h_done, b * FF_UNITS + n + 1)
                copy(h_hi[:, n, :], h_full[:, n % RING, :]).then_inc(h_hi_done, 1)

            def mlp_units(b, units):
                for n in units:
                    gate_tanh(b, n)
                    if n > 0:
                        h_first(b, n - 1)

            def yT_first(b):
                act.wait_ge(yT_full, b + 1)
                copy(yT_hi[:, :, :], misc[:, :].rearrange("p (k t) -> p k t", k=DK)).then_inc(yT_hi_done, 1)

            def residual(b):
                act.wait_ge(x1_done, (b + 1) * TT)
                if not is_first(b):
                    act.wait_ge(out_done, b * TT)
                copy(z2[:, :, :], x1[:, :, :]).then_inc(residual_done, 1)

            def first_norm(b):
                act.wait_ge(attn_step, (b + 1) * ATTN_STEPS)
                if not is_first(b):
                    act.wait_ge(residual_done, b)
                for t in range(TT):
                    act.activation(x1[:, t, :], z1[:, t, :], ACT.Identity, bias=ln_shift[:, t:t + 1],
                                   scale=ln_t[:, 0, 1, t:t + 1]).then_inc(x1_done, 1)

            def x1T_first(b):
                act.wait_ge(x1T_full, b + 1)
                copy(x1T_hi[:, :, :], misc[:, :].rearrange("p (k t) -> p k t", k=DK)).then_inc(x1T_hi_done, 1)

            def router(b, bank=ff[0]):
                act.wait_ge(logitT_full, b + 1)
                copy(logitT[:, :], bank[0:ROUTED, 0:T]).then_inc(logitT_done, 1)

            def router_exp(b):
                act.wait_ge(router_step, b * ROUTER_STEPS + 1)
                act.activation(comb[:, 1, :], comb[:, 0, :], ACT.Exp).then_inc(top_exp_done, 1)

            def copy_shared(b):
                act.wait_ge(shared_full, b + 1)
                copy(shared_out, ff[1][:, :].rearrange("p (t d) -> p t d", t=TT)).then_inc(shared_copied, 1)

            def scale_routed(b):
                act.wait_ge(routed_full, b + 1)
                act.wait_ge(router_step, (b + 1) * ROUTER_STEPS)
                for t in range(TT):
                    act.activation(routed_out[:, t, :], ff[0][:, t * D:(t + 1) * D], ACT.Copy,
                                   scale=comb[:, 5, t:t + 1]).then_inc(routed_copied, 1)

            def iteration(i, has_next=True, has_prev=True, has_last=True):
                if has_next:
                    split_xt(i + 1)
                    for p in range(2):
                        act.wait_ge(parts_stored[p], (i + 1) * (16 * QK_JOBS))
                for u in range(S_UNITS):
                    if is_first(i) and u == QK_AT + 3:
                        for n, (k, cols, raw) in enumerate(GU_PIECES):
                            split_weight(wg_hi[:, k, cols], raw, wg_loaded[n], mlp_w_hi_done)
                    if has_next:
                        if u == QK_AT:
                            first_part(i + 1, 0)
                        if u == QK_AT + 2:
                            second_part(i + 1, 0)
                    if has_prev:
                        if u == APPLY_AT:
                            first_norm(i - 1)
                        if u == X1T_AT:
                            x1T_first(i - 1)
                        if u == ROUTER_AT:
                            router(i - 1)
                        if u == LOGIT_AT + 1:
                            router_exp(i - 1)
                    if has_last:
                        if u == SHARED_AT[-1]:
                            copy_shared(i - 2)
                        if u == ROUTED_AT:
                            scale_routed(i - 2)
                if has_prev:
                    mlp_units(i - 1, (FF_FIRST,))
                max_first(i)
                if has_prev:
                    mlp_units(i - 1, FF_MAX)
                if is_first(i):
                    act.wait_ge(mlp_w_lo_done, 1)
                exps(i, 0)
                if has_prev:
                    h_first(i - 1, FF_MAX[-1])
                exps(i, 1)
                if has_prev:
                    gate_tanh(i - 1, FF_SCORES)
                for g in range(2, GROUPS):
                    exps(i, g)
                if is_first(i):
                    for n, (units, raw) in enumerate(DOWN_PIECES):
                        split_weight(wd_hi[:, units, :], raw, wd_loaded[n], mlp_w_hi_done)
                if has_prev:
                    residual(i - 1)
                    mlp_units(i - 1, (FF_Y0,))
                    mlp_units(i - 1, (FF_Y1,))
                if has_next:
                    values(i + 1, 0)
                yT_first(i)
                if has_prev:
                    mlp_units(i - 1, (FF_YT,))
                if has_next:
                    values(i + 1, 1)
                if has_prev:
                    h_first(i - 1, FF_UNITS - 1)

            def split_weight(hi, raw, loaded, done=w_hi_done):
                act.wait_ge(loaded, 16)
                copy(hi, raw).then_inc(done, 1)

            split_xt(0)
            for c in range(QK_JOBS):
                split_weight(wp_hi[:, :, proj_chunk(c)], wp_raw[:, :, proj_chunk(c)], wp_loaded[c])
                if c > 0:
                    first_part(0, c - 1)
            split_weight(wp_hi[:, :, proj_chunk(QK_JOBS)], wp_raw[:, :, proj_chunk(QK_JOBS)], wp_loaded[QK_JOBS])
            second_part(0, 0)
            first_part(0, QK_JOBS - 1)
            for n in range(1, QK_JOBS):
                second_part(0, n)
            act.wait_ge(consts_made, CONSTS)
            for t in range(TT):
                values(0, t)
            split_weight(wo_hi[:, :, :], wo_raw, wo_loaded)
            split_weight(wr_hi[:, :, :], wr_raw, wr_loaded)
            iteration(0, has_prev=False, has_last=False)
            iteration(1, has_last=False)
            with act.Fori(2, B - 1) as i:
                iteration(i)
            iteration(B - 1, has_next=False)
            first_norm(B - 1)
            x1T_first(B - 1)
            router(B - 1, ybank[1])
            mlp_units(B - 1, range(1))
            router_exp(B - 1)
            mlp_units(B - 1, range(1, FF_UNITS))
            residual(B - 1)
            h_first(B - 1, FF_UNITS - 1)

        @block.tensor
        def _(pe):
            def product(o, lhs_hi, lhs_lo, rhs_hi, rhs_lo, first, last):
                pe.matmul(o, lhs_lo, rhs_hi, start=first, stop=False)
                pe.matmul(o, lhs_hi, rhs_lo, start=False, stop=False)
                return pe.matmul(o, lhs_hi, rhs_hi, start=False, stop=last)

            def qk_job(b, n):
                if n == 0:
                    pe.wait_ge(xt_hi_done, b + 1)
                    pe.wait_ge(xt_lo_done, b + 1)
                if is_first(b):
                    pe.wait_ge(w_hi_done, n + 1)
                    pe.wait_ge(w_lo_done, n + 1)
                elif n == QK_JOBS - 1:
                    pe.wait_ge(max_l_done, b)
                elif not isinstance(b, int) or b > 1:
                    if n == 0:
                        pe.wait_ge(z1_done, b - 1)
                    else:
                        pe.wait_ge(y2_done, (b - 1) * TT)
                for h in range(2):
                    f = slice((2 * n + h) * P, (2 * n + h + 1) * P)
                    for k in range(DK):
                        mm = product(qk_bank(n)[:, h * T:(h + 1) * T], wp_hi[:, k, f], wp_lo[:, k, f],
                                     xt_hi[:, k, :], xt_lo[:, k, :], k == 0, k == DK - 1)
                mm.then_inc(qk_full, 1)

            def v_job(b, t):
                q = slice(t * P, (t + 1) * P)
                w = slice(3 * D, PROJ_COLS)
                for k in range(DK):
                    mm = product(ring[1 + t][:, 0:D + HEADS], xt_hi[:, k, q], xt_lo[:, k, q], wp_hi[:, k, w], wp_lo[:, k, w],
                                 k == 0, k == DK - 1)
                mm.then_inc(v_full, 1)

            def k_head(rows, h, tokens):
                return k_stack[rows, h % BLOCK_HEADS, h // BLOCK_HEADS, tokens]

            def q_head(rows, h, tokens):
                return q_stack[rows, h % BLOCK_HEADS, h // BLOCK_HEADS, tokens]

            def q_pair(rows, n, tokens):
                h = 2 * n
                return q_stack[rows, h % BLOCK_HEADS:h % BLOCK_HEADS + 2, h // BLOCK_HEADS, tokens]

            def s_unit(b, u):
                if u == 0:
                    if not is_first(b):
                        pe.wait_ge(exp_done, b * T_UNITS - RING + 1)
                elif u < RING:
                    pe.wait_ge(v_done, b * TT + u)
                else:
                    pe.wait_ge(max_done, b * S_UNITS + u - RING + 1)
                bank = ring[u % RING]
                if u < QHEADS // 4:
                    t, heads, keys = 0, range(4 * u, 4 * u + 4), P
                else:
                    n = u - QHEADS // 4
                    t, heads, keys = 1, range(2 * n, 2 * n + 2), T
                o = bank[:, :].rearrange("p (h k) -> p h k", k=keys)
                pe.matmul(o[:, :, keys - P:keys], ident_b[:, :], mask_b[:, :].unsqueeze(1).to_broadcast([P, len(heads), P]),
                          start=True, stop=False, skip_group_check=True)
                for j, h in enumerate(heads):
                    mm = pe.matmul(o[:, j, :], q_head(slice(0, STACK_ROWS), h, slice(t * P, (t + 1) * P)), k_head(slice(0, STACK_ROWS), h // 2, slice(0, keys)),
                                   start=False, stop=True, skip_group_check=True)
                mm.then_inc(s_full, 1)

            def max_job(b, has_prev):
                pe.wait_ge(max_done, b * S_UNITS + S_UNITS)
                if has_prev:
                    pe.wait_ge(x1T_lo_done, b)
                for t in range(TT):
                    mm = pe.transpose(misc[0:QHEADS, t * P:(t + 1) * P], neg_max[:, t, :], ident[:, :])
                mm.then_inc(maxT_full, 1)

            def t_group(b, g):
                rows = slice(0, STACK_ROWS + MAX_PARTS)
                for u in range(3):
                    if g == 0:
                        pe.wait_ge(max_done, b * S_UNITS + S_UNITS - RING + u + 1)
                    else:
                        pe.wait_ge(exp_done, b * T_UNITS + 3 * (g - 1) + u + 1)
                    if u < 2:
                        n = 2 * g + u
                        mm = pe.matmul(ring[u][:, :].rearrange("p (h q) -> p h q", h=2), k_head(rows, n, slice(0, P)),
                                       q_pair(rows, n, slice(0, T)), start=True, stop=True)
                    else:
                        for j in range(2):
                            n = 2 * g + j
                            mm = pe.matmul(ring[u][:, j * T:(j + 1) * T].rearrange("p (h q) -> p h q", h=2), k_head(rows, n, slice(P, T)),
                                           q_pair(rows, n, slice(P, T)), start=True, stop=True)
                    mm.then_inc(t_full, 1)

            def pv_group(b, g, has_next):
                bank = ybank[g % 2]
                if g >= 2:
                    pe.wait_ge(yv_done, b * GROUPS + g - 1)
                elif has_next:
                    pe.wait_ge(qk_rest_done, (b + 1) * QK_JOBS + g + 1)
                elif g == 0:
                    pe.wait_ge(z1_done, b)
                else:
                    pe.wait_ge(y2_done, b * TT)
                for t in range(TT):
                    pe.wait_ge(causal_done, b * (2 * GROUPS) + 2 * g + t + 1)
                    for j in range(4):
                        if t == 0:
                            p = prob[:, g % RING, j // 2, (j % 2) * T:(j % 2 + 1) * T]
                        else:
                            p = prob[:, g % RING, 2, j * P:(j + 1) * P]
                        mm = pe.matmul(bank[V_COLS * j:V_COLS * (j + 1), t * P:T], v_ones[:, t, 2 * g + j // 2, :], p,
                                       start=(t == 0), stop=(t == TT - 1))
                mm.then_inc(pv_full, 1)

            def y_jobs(b, t):
                for k, (done, full) in enumerate(((y1_done, y1_full), (y2_done, y2_full))):
                    if t == 0:
                        pe.wait_ge(yv_done, b * GROUPS + (k + 1) * (GROUPS // 2))
                        pe.wait_ge(yv_done, b * GROUPS + GROUPS - 1 + k)
                    else:
                        pe.wait_ge(done, b * TT + t)
                    for j in range(4):
                        mm = pe.transpose(ybank[k][:, j * P:(j + 1) * P], yv[:, 4 * k + j, t * P:(t + 1) * P], ident[:, :])
                    mm.then_inc(full, 1)

            def yT_job(b, has_next):
                if has_next:
                    pe.wait_ge(qk_rest_done, (b + 2) * QK_JOBS)
                else:
                    pe.wait_ge(max_l_done, b + 1)
                for t in range(TT):
                    pe.wait_ge(y_done, b * TT + t + 1)
                    for k in range(DK):
                        mm = pe.transpose(misc[:, k * T + t * P:k * T + (t + 1) * P], y1[:, t, k * P:(k + 1) * P], ident[:, :])
                mm.then_inc(yT_full, 1)

            def wo_job(b):
                pe.wait_ge(yT_hi_done, b + 1)
                pe.wait_ge(yT_lo_done, b + 1)
                pe.wait_ge(y1_done, (b + 1) * TT)
                if is_first(b):
                    pe.wait_ge(w_hi_done, W_OUT)
                    pe.wait_ge(w_lo_done, W_OUT)
                for t in range(TT):
                    q = slice(t * P, (t + 1) * P)
                    for k in range(DK):
                        mm = product(ybank[0][:, t * D:(t + 1) * D], yT_hi[:, k, q], yT_lo[:, k, q], wo_hi[:, k, :], wo_lo[:, k, :],
                                     k == 0, k == DK - 1)
                mm.then_inc(wo_full, 1)

            def x1T_job(b):
                pe.wait_ge(yT_lo_done, b + 1)
                for t in range(TT):
                    pe.wait_ge(x1_done, b * TT + t + 1)
                    for k in range(DK):
                        mm = pe.transpose(misc[:, k * T + t * P:k * T + (t + 1) * P], x1[:, t, k * P:(k + 1) * P], ident[:, :])
                mm.then_inc(x1T_full, 1)

            def gu_units(b, units, router_first=True):
                for n in units:
                    if n == 0:
                        pe.wait_ge(x1T_hi_done, b + 1)
                        pe.wait_ge(x1T_lo_done, b + 1)
                        if router_first:
                            if not is_first(b):
                                pe.wait_ge(routed_copied, b * TT)
                            pe.wait_ge(logitT_done, b + 1)
                    if n == 1:
                        if router_first:
                            pe.wait_ge(top_done, (b + 1) * TT)
                        else:
                            pe.wait_ge(z2_shared_done, b)
                    if n > 1:
                        pe.wait_ge(h_done, b * FF_UNITS + n - 1)
                    if is_first(b) and n == 0:
                        pe.wait_ge(mlp_w_lo_done, W_GATE_UP)
                    for j in range(2):
                        f = slice((2 * n + j) * P, (2 * n + j + 1) * P)
                        for k in range(DK):
                            mm = product(ff[n % 2][:, j * T:(j + 1) * T], wg_hi[:, k, f], wg_lo[:, k, f], x1T_hi[:, k, :], x1T_lo[:, k, :],
                                         k == 0, k == DK - 1)
                    mm.then_inc(gu_full, 1)

            def router_job(b, bank=ff[0]):
                pe.wait_ge(x1T_hi_done, b + 1)
                pe.wait_ge(x1T_lo_done, b + 1)
                if not is_first(b):
                    pe.wait_ge(h_done, b * FF_UNITS)
                else:
                    pe.wait_ge(w_hi_done, W_ROUTER)
                    pe.wait_ge(w_lo_done, W_ROUTER)
                for k in range(DK):
                    mm = product(bank[:, 0:T], wr_hi[:, k, :], wr_lo[:, k, :], x1T_hi[:, k, :], x1T_lo[:, k, :], k == 0, k == DK - 1)
                mm.then_inc(logitT_full, 1)

            def logit_job(b, bank=ff[1]):
                if not is_first(b) and bank is ff[1]:
                    pe.wait_ge(shared_copied, b)
                pe.wait_ge(logitT_done, b + 1)
                own_wait(pe)
                for t in range(TT):
                    mm = pe.transpose(bank[:, t * ROUTED:(t + 1) * ROUTED], logitT[:, t * P:(t + 1) * P], ident[0:ROUTED, 0:ROUTED])
                mm.then_inc(logit_full, 1)

            def down(bank, t, units, first, last):
                for n in units:
                    q = slice(t * P, (t + 1) * P)
                    mm = product(bank[:, t * D:(t + 1) * D], h_hi[:, n, q], h_lo[:, n, q], wd_hi[:, n, :], wd_lo[:, n, :],
                                 n == first, n == last)
                return mm

            def shared_chunk(b, c, bank=ff[1]):
                half = SHARED_UNITS * TT // DOWN_CHUNKS
                t, n = divmod(c * half, SHARED_UNITS)
                if bank is ff[1] and c == 0:
                    pe.wait_ge(h_lo_done, (b + 1) * FF_UNITS)
                elif bank is not ff[1]:
                    pe.wait_ge(h_lo_done, b * FF_UNITS + n + half)
                mm = down(bank, t, range(n, n + half), 0, SHARED_UNITS - 1)
                if c == DOWN_CHUNKS - 1:
                    mm.then_inc(shared_full, 1)

            def routed_job(b, bank=ff[0]):
                if bank is ff[0]:
                    pe.wait_ge(logitT_done, b + 2)
                else:
                    pe.wait_ge(h_lo_done, (b + 1) * FF_UNITS)
                for t in range(TT):
                    mm = down(bank, t, range(SHARED_UNITS, FF_UNITS), SHARED_UNITS, FF_UNITS - 1)
                mm.then_inc(routed_full, 1)

            def iteration(i, has_next=True, has_prev=True, has_last=True):
                pe.wait_ge(stack_loaded, (i + 1) * (16 * STACK_LOADS))
                for u in range(S_UNITS):
                    s_unit(i, u)
                    if has_next and u == QK_AT:
                        qk_job(i + 1, 0)
                    if has_last and u in SHARED_AT:
                        shared_chunk(i - 2, SHARED_AT.index(u))
                    if has_prev and u == X1T_AT:
                        x1T_job(i - 1)
                    if has_prev and u == ROUTER_AT:
                        router_job(i - 1)
                    if has_last and u == ROUTED_AT:
                        routed_job(i - 2)
                    if has_prev and u == LOGIT_AT:
                        logit_job(i - 1)
                if has_prev:
                    gu_units(i - 1, (FF_FIRST,))
                max_job(i, has_prev)
                if has_prev:
                    gu_units(i - 1, FF_MAX)
                pe.wait_ge(max_loaded, (i + 1) * (16 * MAX_PARTS))
                for g in range(GROUPS + 2):
                    if g < GROUPS:
                        t_group(i, g)
                    if g == FF_SCORES_GROUP and has_prev:
                        gu_units(i - 1, (FF_SCORES,))
                    if g >= 2:
                        pv_group(i, g - 2, has_next)
                    if has_next and g in QK_GROUPS:
                        qk_job(i + 1, 1 + QK_GROUPS.index(g))
                y_jobs(i, 0)
                if has_prev:
                    gu_units(i - 1, (FF_Y0,))
                y_jobs(i, 1)
                if has_prev:
                    gu_units(i - 1, (FF_Y1,))
                if has_next:
                    v_job(i + 1, 0)
                yT_job(i, has_next)
                if has_prev:
                    gu_units(i - 1, (FF_YT,))
                if has_next:
                    v_job(i + 1, 1)
                wo_job(i)

            for n in range(QK_JOBS):
                qk_job(0, n)
            pe.wait_ge(w_hi_done, W_PROJ)
            pe.wait_ge(w_lo_done, W_PROJ)
            for t in range(TT):
                v_job(0, t)
            pe.wait_ge(consts_made, CONSTS)
            iteration(0, has_prev=False, has_last=False)
            iteration(1, has_last=False)
            pe.wait_ge(mlp_w_lo_done, W_DOWN)
            with pe.Fori(2, B - 1) as i:
                iteration(i)
            iteration(B - 1, has_next=False)
            for c in range(DOWN_CHUNKS - 1):
                shared_chunk(B - 2, c)
            routed_job(B - 2, ring[1])
            x1T_job(B - 1)
            shared_chunk(B - 2, DOWN_CHUNKS - 1)
            router_job(B - 1, ybank[1])
            gu_units(B - 1, range(0, 1), router_first=False)
            logit_job(B - 1, ybank[0])
            gu_units(B - 1, range(1, FF_UNITS), router_first=False)
            for c in range(DOWN_CHUNKS):
                shared_chunk(B - 1, c, ring[0])
            routed_job(B - 1, ring[2])

        @block.vector
        def _(dve):
            def stepper(semaphore, done):
                count = [done]

                def step(ins):
                    count[0] = count[0] + 1
                    ins.then_inc(semaphore, 1)

                def settle():
                    dve.wait_ge(semaphore, count[0])
                return step, settle

            def norm_stats(which, z, step, settle):
                for t in range(TT):
                    step(dve.bn_stats(ln_stats[:, which, t, :], z[:, t, :]))

            def norm_mean(which, step, settle):
                settle()
                own_wait(dve)
                for t in range(TT):
                    step(dve.bn_aggr(ln_mv[:, which, t, :], ln_stats[:, which, t, :]))

            def norm_half(which, step, settle):
                settle()
                step(dve.tensor_scalar(ln_t[:, which, 0, :], ln_mv[:, which, :, 1], EPS, 0.5, ALU.add, ALU.mult))

            def norm_seed(which, step, settle):
                seed = ln_i[:, which, :]
                settle()
                step(dve.tensor_scalar(seed, ln_t[:, which, 0, :].bitcast(I32), 1, None, ALU.logical_shift_right))
                settle()
                step(dve.tensor_scalar(ln_t[:, which, 1, :].bitcast(I32), seed, -1.0, RSQRT_SEED, ALU.mult, ALU.add))

            def norm_newton(which, step, settle):
                half_var, r, a = ln_t[:, which, 0, :], ln_t[:, which, 1, :], ln_t[:, which, 2, :]
                settle()
                for t in range(TT):
                    step(dve.scalar_tensor_tensor(a[:, t:t + 1], r[:, t:t + 1], r[:, t:t + 1], half_var[:, t:t + 1], ALU.mult, ALU.mult))
                settle()
                step(dve.scalar_tensor_tensor(r, a, 1.5, r, ALU.subtract, ALU.mult, reverse0=True))

            def first_norm_step(n, step, settle):
                if n == 0:
                    norm_mean(0, step, settle)
                elif n == 1:
                    norm_half(0, step, settle)
                elif n == 2:
                    norm_seed(0, step, settle)
                elif n < NEWTON + 3:
                    norm_newton(0, step, settle)
                else:
                    settle()
                    step(dve.scalar_tensor_tensor(ln_shift[:, :], ln_mv[:, 0, :, 0], -1.0, ln_t[:, 0, 1, :], ALU.mult, ALU.mult))

            def split_xt(b):
                dve.wait_ge(xt_hi_done, b + 1)
                dve.tensor_tensor(xt_lo[:, :, :], xt_raw[:, :, :], xt_hi[:, :, :].bitcast(F32), ALU.subtract).then_inc(xt_lo_done, 1)

            def qk_rest(b, n):
                dve.wait_ge(qk_h_done, b * QK_JOBS + n + 1)
                dve.tensor_tensor(rest[:, n, :].rearrange("p (b t) -> p b t", b=2), qk_bank(n)[:, :].rearrange("p (b t) -> p b t", b=2),
                                  parts[:, 0, 2 * n:2 * n + 2, :], ALU.subtract).then_inc(qk_rest_done, 1)

            def qk_split(b, n):
                view = "p (b t) -> p b t"
                dve.wait_ge(qk_full, b * QK_JOBS + n + 1)
                dve.tensor_copy(parts[:, 0, 2 * n:2 * n + 2, :], qk_bank(n)[:, :].rearrange(view, b=2)).then_inc(qk_h_done, 1)
                qk_rest(b, n)
                dve.wait_ge(qk_rest_done, b * QK_JOBS + n + 1)
                dve.tensor_copy(parts[:, 1, 2 * n:2 * n + 2, :], rest[:, n, :].rearrange(view, b=2)).then_inc(qk_m_done, 1)

            def row_max(b, u):
                dve.wait_ge(s_full, b * S_UNITS + u + 1)
                if u < QHEADS // 4:
                    o, keys = neg_max[:, 0, 4 * u:4 * u + 4], P
                else:
                    n = u - QHEADS // 4
                    o, keys = neg_max[:, 1, 2 * n:2 * n + 2], T
                dve.tensor_reduce(o, ring[u % RING][:, :].rearrange("p (h k) -> p h k", k=keys), AX_X, ALU.max,
                                  negate=True).then_inc(max_done, 1)

            def max_second(b):
                dve.wait_ge(max_h_done, b + 1)
                dve.tensor_tensor(max_parts[:, 1, :], misc[0:QHEADS, 0:T], max_parts[:, 0, :], ALU.subtract).then_inc(max_l_done, 1)

            def mlp_unit(b, n):
                dve.wait_ge(gate_th_done, b * FF_UNITS + n + 1)
                dve.scalar_tensor_tensor(gate_t[:, n % RING, :], gate_t[:, n % RING, :], 1.0, ff[n % 2][:, 0:T], ALU.add,
                                         ALU.mult).then_inc(gate_done, 1)
                dve.wait_ge(gate_done, b * FF_UNITS + n + 1)
                if n >= RING:
                    dve.wait_ge(h_lo_done, b * FF_UNITS + n - RING + 1)
                dve.scalar_tensor_tensor(h_full[:, n % RING, :], gate_t[:, n % RING, :], 0.5, ff[n % 2][:, T:2 * T], ALU.mult,
                                         ALU.mult).then_inc(h_done, 1)

            def evacuate_pv(b, g):
                dve.wait_ge(pv_full, b * GROUPS + g + 1)
                dve.tensor_copy(yv[:, g, :], ybank[g % 2][:, 0:T]).then_inc(yv_done, 1)

            def normalize_y(b, t, step, settle):
                def heads(bank):
                    return bank[:, :].rearrange("p (h c) -> p h c", c=V_COLS)

                def wide(r):
                    return r.unsqueeze(2).to_broadcast([P, HEADS, HEAD_DIM])

                dve.wait_ge(y1_full, b * TT + t + 1)
                step(dve.reciprocal(recip[:, 0, :], heads(ybank[0])[:, :, HEAD_DIM]))
                dve.wait_ge(y2_full, b * TT + t + 1)
                step(dve.reciprocal(recip[:, 1, :], heads(ybank[1])[:, :, HEAD_DIM]))
                settle()
                step(dve.tensor_tensor(recip[:, 2, :], recip[:, 1, :], lam[:, t, :], ALU.mult))
                view = "p (h d) -> p h d"
                dve.tensor_tensor(y1[:, t, :].rearrange(view, h=HEADS), heads(ybank[0])[:, :, 0:HEAD_DIM], wide(recip[:, 0, :]),
                                  ALU.mult).then_inc(y1_done, 1)
                settle()
                dve.tensor_tensor(y2[:, t, :].rearrange(view, h=HEADS), heads(ybank[1])[:, :, 0:HEAD_DIM], wide(recip[:, 2, :]),
                                  ALU.mult).then_inc(y2_done, 1)
                dve.wait_ge(y1_done, b * TT + t + 1)
                dve.wait_ge(y2_done, b * TT + t + 1)
                dve.tensor_tensor(y1[:, t, :], y1[:, t, :], y2[:, t, :], ALU.subtract).then_inc(y_done, 1)

            def yT_second(b):
                dve.wait_ge(yT_hi_done, b + 1)
                dve.tensor_tensor(yT_lo[:, :, :], misc[:, :].rearrange("p (k t) -> p k t", k=DK), yT_hi[:, :, :].bitcast(F32),
                                  ALU.subtract).then_inc(yT_lo_done, 1)

            def add_input(b):
                dve.wait_ge(wo_full, b + 1)
                dve.wait_ge(x_loaded, (b + 1) * 16)
                dve.tensor_tensor(z1[:, :, :], ybank[0][:, :].rearrange("p (t d) -> p t d", t=TT), x_in[:, :, :], ALU.add).then_inc(z1_done, 1)
                dve.wait_ge(z1_done, b + 1)

            def x1T_second(b):
                dve.wait_ge(x1T_hi_done, b + 1)
                dve.tensor_tensor(x1T_lo[:, :, :], misc[:, :].rearrange("p (k t) -> p k t", k=DK), x1T_hi[:, :, :].bitcast(F32),
                                  ALU.subtract).then_inc(x1T_lo_done, 1)

            def router_top(b, step, bank=ff[1]):
                dve.wait_ge(logit_full, b + 1)
                own_wait(dve)
                for t in range(TT):
                    dve.max(top8[:, t, :], bank[:, t * ROUTED:(t + 1) * ROUTED]).then_inc(top_done, 1)
                dve.wait_ge(top_done, (b + 1) * TT)
                step(dve.tensor_tensor(comb[:, 0, :], top8[:, :, 1], top8[:, :, 0], ALU.subtract))

            def router_sum(b, step, settle):
                dve.wait_ge(top_exp_done, b + 1)
                step(dve.tensor_scalar(comb[:, 2, :], comb[:, 1, :], 1.0, None, ALU.add))
                settle()
                step(dve.reciprocal(comb[:, 3, :], comb[:, 2, :]))
                settle()
                step(dve.tensor_tensor(comb[:, 4, :], comb[:, 1, :], comb[:, 3, :], ALU.mult))
                settle()
                step(dve.tensor_tensor(comb[:, 5, :], comb[:, 3, :], comb[:, 4, :], ALU.add))

            def add_shared(b, bank=ff[1]):
                dve.wait_ge(shared_full, b + 1)
                dve.wait_ge(residual_done, b + 1)
                dve.tensor_tensor(z2[:, :, :], bank[:, :].rearrange("p (t d) -> p t d", t=TT), z2[:, :, :], ALU.add).then_inc(z2_shared_done, 1)

            def add_routed(b, bank=ff[0]):
                dve.wait_ge(routed_full, b + 1)
                dve.wait_ge(z2_shared_done, b + 1)
                dve.wait_ge(router_step, (b + 1) * ROUTER_STEPS)
                for t in range(TT):
                    dve.scalar_tensor_tensor(z2[:, t, :], bank[:, t * D:(t + 1) * D], comb[:, 5, t:t + 1], z2[:, t, :], ALU.mult,
                                             ALU.add).then_inc(z2_done, 1)

            def second_norm_start(b, step, settle):
                dve.wait_ge(z2_done, (b + 1) * TT)
                norm_stats(1, z2, step, settle)
                norm_mean(1, step, settle)
                norm_half(1, step, settle)
                norm_seed(1, step, settle)

            def second_norm_end(b, step, settle):
                if not is_first(b):
                    dve.wait_ge(out_stored, (b + 1) * 16)
                settle()
                for t in range(TT):
                    dve.tensor_scalar(out_t[:, t, :], z2[:, t, :], ln_mv[:, 1, t, 0:1], ln_t[:, 1, 1, t:t + 1], ALU.subtract,
                                      ALU.mult).then_inc(out_done, 1)

            def iteration(i, has_next=True, has_prev=True, has_last=True):
                attn = stepper(attn_step, i * ATTN_STEPS)
                router_steps = stepper(router_step, (i - 1) * ROUTER_STEPS)
                norm2 = stepper(norm2_step, (i - 2) * LN_STEPS)
                if has_next:
                    dve.wait_ge(qk_l_done, (i + 1) * QK_JOBS)
                if has_prev:
                    before = stepper(attn_step, i * ATTN_STEPS - NORM1_STEPS + TT)
                for u in range(S_UNITS):
                    row_max(i, u)
                    if has_prev:
                        if u < NEWTON + 4:
                            first_norm_step(u, *before)
                        if u - 2 == X1T_AT:
                            x1T_second(i - 1)
                        if u - 1 == LOGIT_AT:
                            router_top(i - 1, router_steps[0])
                    if has_next and u - 1 == QK_AT:
                        qk_rest(i + 1, 0)
                if has_prev:
                    mlp_unit(i - 1, FF_FIRST)
                max_second(i)
                attn[0](dve.tensor_scalar(lam[:, :, :], lam_th[:, :, :], 0.5, 0.5, ALU.mult, ALU.add))
                if has_prev:
                    for n in FF_MAX:
                        mlp_unit(i - 1, n)
                        if n == FF_MAX[0]:
                            router_sum(i - 1, *router_steps)
                if has_next:
                    for p in range(2):
                        dve.wait_ge(parts_stored[p], (i + 1) * (16 * QK_JOBS))
                    qk_split(i + 1, 1)
                if has_prev:
                    mlp_unit(i - 1, FF_SCORES)
                for g in range(GROUPS):
                    if g == 0 and is_first(i):
                        dve.wait_ge(mlp_w_lo_done, W_GATE_UP)
                    evacuate_pv(i, g)
                    if has_next and g + 2 == QK_GROUPS[1]:
                        qk_split(i + 1, 2)
                    if has_last:
                        if g == 0:
                            second_norm_start(i - 2, *norm2)
                        elif g <= NEWTON:
                            norm_newton(1, *norm2)
                        elif g == NEWTON + 1:
                            second_norm_end(i - 2, *norm2)
                normalize_y(i, 0, *attn)
                if has_prev:
                    mlp_unit(i - 1, FF_Y0)
                normalize_y(i, 1, *attn)
                if has_prev:
                    mlp_unit(i - 1, FF_Y1)
                yT_second(i)
                if has_prev:
                    mlp_unit(i - 1, FF_YT)
                add_input(i)
                norm_stats(0, z1, *attn)

            def split_weight(n, lo, raw, hi):
                dve.wait_ge(w_hi_done, n)
                dve.tensor_tensor(lo, raw, hi.bitcast(F32), ALU.subtract).then_inc(w_lo_done, 1)

            split_xt(0)
            for c in range(QK_JOBS):
                split_weight(c + 1, wp_lo[:, :, proj_chunk(c)], wp_raw[:, :, proj_chunk(c)], wp_hi[:, :, proj_chunk(c)])
                if c > 0:
                    qk_rest(0, c - 1)
            split_weight(W_PROJ, wp_lo[:, :, proj_chunk(QK_JOBS)], wp_raw[:, :, proj_chunk(QK_JOBS)], wp_hi[:, :, proj_chunk(QK_JOBS)])
            qk_rest(0, QK_JOBS - 1)
            split_weight(W_OUT, wo_lo[:, :, :], wo_raw, wo_hi[:, :, :])
            split_weight(W_ROUTER, wr_lo[:, :, :], wr_raw, wr_hi[:, :, :])
            iteration(0, has_prev=False, has_last=False)
            iteration(1, has_last=False)
            with dve.Fori(2, B - 1) as i:
                iteration(i)
            iteration(B - 1, has_next=False)

            first = stepper(attn_step, B * ATTN_STEPS - NORM1_STEPS + TT)
            for n in range(NEWTON + 4):
                first_norm_step(n, *first)
            x1T_second(B - 1)
            add_shared(B - 2)
            add_routed(B - 2, ring[1])
            last_router = stepper(router_step, (B - 1) * ROUTER_STEPS)
            router_top(B - 1, last_router[0], ybank[0])
            norm2 = stepper(norm2_step, (B - 2) * LN_STEPS)
            for n in range(FF_UNITS):
                mlp_unit(B - 1, n)
                if n == 0:
                    router_sum(B - 1, *last_router)
                if n == 1:
                    second_norm_start(B - 2, *norm2)
                if 1 < n < NEWTON + 2:
                    norm_newton(1, *norm2)
                if n == NEWTON + 2:
                    second_norm_end(B - 2, *norm2)
            add_shared(B - 1, ring[0])
            add_routed(B - 1, ring[2])
            norm2 = stepper(norm2_step, (B - 1) * LN_STEPS)
            second_norm_start(B - 1, *norm2)
            for _ in range(NEWTON):
                norm_newton(1, *norm2)
            second_norm_end(B - 1, *norm2)


_OUT = ((B, T, D), "float32")


def kernel(**inputs):
    import numpy as np
    import concourse.bacc as bacc
    from concourse.bass_utils import run_bass_kernel_spmd

    a = {n[len("L0_"):]: np.asarray(v) for n, v in inputs.items()}
    gate = np.concatenate([a["ffn_sh_gate"], a["ffn_r_gate"]]).reshape(FF_UNITS, 1, P, D)
    up = np.concatenate([a["ffn_sh_up"], a["ffn_r_up"]]).reshape(FF_UNITS, 1, P, D)
    arrays = {
        "x": a["attn_x"],
        "xT": a["attn_x"].transpose(0, 2, 1),
        "w_proj": np.concatenate([a["attn_Wq1"], a["attn_Wq2"], a["attn_Wk"], a["attn_Wv"], a["attn_Wlam"]], axis=1),
        "w_out": a["attn_Wo"],
        "w_gu": np.concatenate([gate, up], axis=1).reshape(2 * FF_UNITS * P, D).T,
        "w_down": np.concatenate([a["ffn_sh_down"], a["ffn_r_down"]], axis=1).T,
        "w_router": a["ffn_router_weight"].T,
    }
    arrays = {n: np.ascontiguousarray(v) for n, v in arrays.items()}
    nc = bacc.Bacc("TRN2", target_bir_lowering=False, num_devices=1)
    args = {n: nc.dram_tensor(n, v.shape, mybir.dt.from_np(v.dtype), kind="ExternalInput").ap() for n, v in arrays.items()}
    out = nc.dram_tensor("out", _OUT[0], F32, kind="ExternalOutput").ap()
    build_layer(nc, out=out, **args)
    return run_bass_kernel_spmd(nc, [arrays], core_ids=[0]).results[0]["out"]
```
